# Optimizing a Trainium2 kernel written in Bass

```python
import numpy as np
import jax
import jax.numpy as jnp

def _softmax(x, axis=-1):
    return jax.nn.softmax(x, axis=axis)

def _gelu(x):
    return jax.nn.gelu(x, approximate=True)

def _silu(x):
    return jax.nn.silu(x)

def _sigmoid(x):
    return jax.nn.sigmoid(x)

def _layernorm(x, axis=-1, eps=1e-05):
    m = jnp.mean(x, axis=axis, keepdims=True)
    v = jnp.var(x, axis=axis, keepdims=True)
    return (x - m) / jnp.sqrt(v + eps)

def _scatter_add(tgt, idx, src, axis=0):
    return tgt.at[idx].add(src)

def _segment_sum(src, seg, n):
    return jax.ops.segment_sum(src, seg, n)
kernel_name = 'mk_hybrid_d1_jaxref_r8_f90019'

def setup_inputs(seed: int=0):
    np.random.seed(seed)
    _w = jnp.asarray

    def _L0_attn_a_setup():
        import jax, jax.numpy as jnp
        import numpy as np
        import math
        D_MODEL = 128
        NUM_HEADS = 16
        HEAD_DIM = D_MODEL // NUM_HEADS
        key = jax.random.key(seed)
        k_x, k_qkv, k_o = jax.random.split(key, 3)
        B, S = (2, 256)
        x = jax.random.normal(k_x, (B, S, D_MODEL), dtype=jnp.float32)
        sigma_qkv = math.sqrt(2.0 / (D_MODEL + 3 * D_MODEL))
        w_qkv = jax.random.truncated_normal(k_qkv, -3.0, 3.0, (3 * D_MODEL, D_MODEL), dtype=jnp.float32) * sigma_qkv
        sigma_o = math.sqrt(2.0 / (D_MODEL + D_MODEL))
        w_out = jax.random.truncated_normal(k_o, -3.0, 3.0, (D_MODEL, D_MODEL), dtype=jnp.float32) * sigma_o
        return {'x': x, 'w_qkv': w_qkv, 'w_out': w_out}
    _L0_attn_a_in = _L0_attn_a_setup()

    def _L0_attn_b_setup():
        import jax, jax.numpy as jnp
        import numpy as np
        D_MODEL = 128
        N_HEADS = 16
        D_HIDDEN = 512
        BATCH = 2
        N_CTX = 256

        def _split_heads(t, n_heads):
            B, S, D = t.shape
            return t.reshape(B, S, n_heads, D // n_heads).transpose(0, 2, 1, 3)
        key = jax.random.key(seed)
        ks = jax.random.split(key, 4)
        scale = 0.02
        x = jax.random.normal(ks[0], (BATCH, N_CTX, D_MODEL), dtype=jnp.float32)
        Wk = jax.random.normal(ks[1], (D_MODEL, D_MODEL), dtype=jnp.float32) * scale
        bk = jnp.zeros((D_MODEL,), dtype=jnp.float32)
        Wv = jax.random.normal(ks[2], (D_MODEL, D_HIDDEN), dtype=jnp.float32) * scale
        bv = jnp.zeros((D_HIDDEN,), dtype=jnp.float32)
        Wf = jax.random.normal(ks[3], (D_HIDDEN, D_MODEL), dtype=jnp.float32) * scale
        bf = jnp.zeros((D_MODEL,), dtype=jnp.float32)
        return {'x': x, 'Wk': Wk, 'bk': bk, 'Wv': Wv, 'bv': bv, 'Wf': Wf, 'bf': bf}
    _L0_attn_b_in = _L0_attn_b_setup()

    def _L0_ffn_setup():
        import jax, jax.numpy as jnp
        import numpy as np
        D_MODEL = 128
        HIDDEN = 512
        N_ROUTING = 2
        key = jax.random.key(seed)
        ks = jax.random.split(key, 10)
        s = 0.02
        x = jax.random.normal(ks[0], (4, 512, D_MODEL), dtype=jnp.float32)
        gate_w = jax.random.normal(ks[1], (N_ROUTING, D_MODEL), dtype=jnp.float32) * s
        w1 = jax.random.normal(ks[2], (N_ROUTING, D_MODEL, HIDDEN), dtype=jnp.float32) * s
        b1 = jax.random.normal(ks[3], (N_ROUTING, HIDDEN), dtype=jnp.float32) * s
        w2 = jax.random.normal(ks[4], (N_ROUTING, HIDDEN, D_MODEL), dtype=jnp.float32) * s
        b2 = jax.random.normal(ks[5], (N_ROUTING, D_MODEL), dtype=jnp.float32) * s
        sw1 = jax.random.normal(ks[6], (D_MODEL, HIDDEN), dtype=jnp.float32) * s
        sb1 = jax.random.normal(ks[7], (HIDDEN,), dtype=jnp.float32) * s
        sw2 = jax.random.normal(ks[8], (HIDDEN, D_MODEL), dtype=jnp.float32) * s
        sb2 = jax.random.normal(ks[9], (D_MODEL,), dtype=jnp.float32) * s
        return {'x': x, 'gate_w': gate_w, 'w1': w1, 'b1': b1, 'w2': w2, 'b2': b2, 'sw1': sw1, 'sb1': sb1, 'sw2': sw2, 'sb2': sb2}
    _L0_ffn_in = _L0_ffn_setup()
    _d = {'L0_attn_a_x': _L0_attn_a_in['x'], 'L0_attn_a_w_qkv': _L0_attn_a_in['w_qkv'], 'L0_attn_a_w_out': _L0_attn_a_in['w_out'], 'L0_attn_b_Wk': _L0_attn_b_in['Wk'], 'L0_attn_b_bk': _L0_attn_b_in['bk'], 'L0_attn_b_Wv': _L0_attn_b_in['Wv'], 'L0_attn_b_bv': _L0_attn_b_in['bv'], 'L0_attn_b_Wf': _L0_attn_b_in['Wf'], 'L0_attn_b_bf': _L0_attn_b_in['bf'], 'L0_ffn_gate_w': _L0_ffn_in['gate_w'], 'L0_ffn_w1': _L0_ffn_in['w1'], 'L0_ffn_b1': _L0_ffn_in['b1'], 'L0_ffn_w2': _L0_ffn_in['w2'], 'L0_ffn_b2': _L0_ffn_in['b2'], 'L0_ffn_sw1': _L0_ffn_in['sw1'], 'L0_ffn_sb1': _L0_ffn_in['sb1'], 'L0_ffn_sw2': _L0_ffn_in['sw2'], 'L0_ffn_sb2': _L0_ffn_in['sb2']}
    _x0 = _d['L0_attn_a_x']
    _d['L0_attn_a_x'] = jax.random.normal(jax.random.fold_in(jax.random.key(seed), 1), (1, 2048, 128), dtype=_x0.dtype)
    del _x0
    return _d

def reference(L0_attn_a_x, L0_attn_a_w_qkv, L0_attn_a_w_out, L0_attn_b_Wk, L0_attn_b_bk, L0_attn_b_Wv, L0_attn_b_bv, L0_attn_b_Wf, L0_attn_b_bf, L0_ffn_gate_w, L0_ffn_w1, L0_ffn_b1, L0_ffn_w2, L0_ffn_b2, L0_ffn_sw1, L0_ffn_sb1, L0_ffn_sw2, L0_ffn_sb2):

    def _L0_attn_a_ref(x, w_qkv, w_out):
        import jax, jax.numpy as jnp
        import numpy as np
        import math
        D_MODEL = 128
        NUM_HEADS = 16
        HEAD_DIM = D_MODEL // NUM_HEADS
        B, S, _ = x.shape
        qkv = jnp.einsum('bsi,oi->bso', x, w_qkv)
        q, k, v = jnp.split(qkv, 3, axis=-1)

        def to_heads(t):
            return t.reshape(B, S, NUM_HEADS, HEAD_DIM).transpose(0, 2, 1, 3)
        q, k, v = (to_heads(q), to_heads(k), to_heads(v))
        scale = 1.0 / math.sqrt(HEAD_DIM)
        logits = jnp.einsum('bhsd,bhtd->bhst', q, k) * scale
        mask = jnp.tril(jnp.ones((S, S), dtype=bool))
        neg_inf = jnp.finfo(jnp.float32).min
        logits = jnp.where(mask, logits, neg_inf)
        probs = jax.nn.softmax(logits, axis=-1)
        probs = probs * mask.astype(probs.dtype)
        out = jnp.einsum('bhst,bhtd->bhsd', probs, v)
        out = out.transpose(0, 2, 1, 3).reshape(B, S, D_MODEL)
        return jnp.einsum('bsi,oi->bso', out, w_out)

    def _L0_attn_b_ref(x, Wk, bk, Wv, bv, Wf, bf):
        import jax, jax.numpy as jnp
        import numpy as np
        D_MODEL = 128
        N_HEADS = 16
        D_HIDDEN = 512
        BATCH = 2
        N_CTX = 256

        def _split_heads(t, n_heads):
            B, S, D = t.shape
            return t.reshape(B, S, n_heads, D // n_heads).transpose(0, 2, 1, 3)
        B, S, D = x.shape
        H = N_HEADS
        Q = _split_heads(x, H)
        K = _split_heads(x @ Wk + bk, H)
        V = _split_heads(x @ Wv + bv, H)
        causal = jnp.tril(jnp.ones((S, S), dtype=bool))
        mask = jnp.where(causal, 0.0, -jnp.inf).astype(x.dtype)
        scores = jnp.einsum('bhqd,bhkd->bhqk', Q, K) + mask
        attn = jax.nn.softmax(scores, axis=-1)
        o = jnp.einsum('bhqk,bhkd->bhqd', attn, V)
        o = o.transpose(0, 2, 1, 3).reshape(B, S, -1)
        return x + jax.nn.gelu(o, approximate=False) @ Wf + bf

    def _L0_ffn_ref(x, gate_w, w1, b1, w2, b2, sw1, sb1, sw2, sb2):
        import jax, jax.numpy as jnp
        import numpy as np
        D_MODEL = 128
        HIDDEN = 512
        N_ROUTING = 2
        B, S, D = x.shape
        xf = x.reshape(-1, D)
        gate_scores = xf @ gate_w.T
        gate_probs = jax.nn.softmax(gate_scores, axis=-1)
        top1 = jnp.argmax(gate_probs, axis=-1)
        one_hot = jax.nn.one_hot(top1, N_ROUTING, dtype=xf.dtype)
        masked = xf[None, :, :] * one_hot.T[:, :, None]
        h = jax.nn.relu(jnp.einsum('end,edh->enh', masked, w1) + b1[:, None, :])
        expert_out = jnp.einsum('enh,ehd->end', h, w2) + b2[:, None, :]
        routing_output = expert_out.sum(axis=0)
        shared = jax.nn.relu(xf @ sw1 + sb1) @ sw2 + sb2
        return (routing_output + shared).reshape(B, S, D)
    x = L0_attn_a_x
    x = x + _L0_attn_a_ref(_layernorm(x, axis=-1), L0_attn_a_w_qkv, L0_attn_a_w_out)
    x = x + _L0_ffn_ref(_layernorm(x, axis=-1), L0_ffn_gate_w, L0_ffn_w1, L0_ffn_b1, L0_ffn_w2, L0_ffn_b2, L0_ffn_sw1, L0_ffn_sb1, L0_ffn_sw2, L0_ffn_sb2)
    x = x + _L0_attn_b_ref(_layernorm(x, axis=-1), L0_attn_b_Wk, L0_attn_b_bk, L0_attn_b_Wv, L0_attn_b_bv, L0_attn_b_Wf, L0_attn_b_bf)
    x = x + _L0_ffn_ref(_layernorm(x, axis=-1), L0_ffn_gate_w, L0_ffn_w1, L0_ffn_b1, L0_ffn_w2, L0_ffn_b2, L0_ffn_sw1, L0_ffn_sb1, L0_ffn_sw2, L0_ffn_sb2)
    return x

_drawn_inputs = setup_inputs


def setup_inputs(seed=0):
    import zlib

    import numpy as np

    out = dict(_drawn_inputs(seed))
    spreads = {'L0_attn_b_bk': (0.0, 0.8), 'L0_attn_b_bv': (0.0, 0.749), 'L0_attn_b_bf': (0.0, 0.1)}
    factors = {'L0_attn_b_Wk': 8.0,
     'L0_attn_b_Wv': 8.0,
     'L0_attn_b_Wf': 4.812,
     'L0_ffn_b1': 4.802,
     'L0_ffn_sb1': 6.141}
    for name, (base, spread) in spreads.items():
        noise = np.random.default_rng([zlib.crc32(name.encode()), seed]).standard_normal(out[name].shape)
        drawn = base * np.exp(spread * noise) if base else spread * noise
        out[name] = jnp.asarray(drawn.astype(out[name].dtype))
    for name, factor in factors.items():
        out[name] = (out[name] * factor).astype(out[name].dtype)
    return out
```

```python
from contextlib import ExitStack

import concourse.bass as bass
import numpy as np
from concourse import mybir

F32 = mybir.dt.float32
BF16 = mybir.dt.bfloat16
ALU = mybir.AluOpType
ACT = mybir.ActivationFunctionType
AX = mybir.AxisListType

P = 128
S = 2048
D = 128
HEADS = 16
HD = D // HEADS
QUAD = 4
QUADS = HEADS // QUAD
TILES = S // P
CHUNK = 512
CHUNKS = S // CHUNK
TPC = CHUNK // P
VW = 32
HID = 512
EXPERTS = 3
HCH = EXPERTS * HID // P
EPS = 1e-5

PAIRS = [(0, 2), (0, 1), (0, 0), (1, 0), (2, 0), (1, 1)]
COMBOS = len(PAIRS)
ROWS = COMBOS * HD
PARTS = 3

UNITS = [(c, kt) for c in range(CHUNKS) for kt in range(TPC * (c + 1))]
NU = len(UNITS)
FIRST = [UNITS.index((c, 0)) for c in range(CHUNKS)] + [NU]
COMBO = [(c, kc, i) for c in range(CHUNKS) for kc in range(c + 1) for i in range(TPC)]
TURN_AT = {FIRST[c + 1] + 2: c for c in range(CHUNKS - 1)}
OUT_AT = {FIRST[c + 1] + 2: c for c in range(CHUNKS - 1)}


def order(kind, with_quad, with_max):
    out = [("den", "out"), ("out",)][kind == "a"]
    steps = []
    for n in range(NU):
        tiles = [("max", n, h) for h in range(QUAD)] if with_max else [None] * QUAD
        if with_max and n in TURN_AT:
            steps.append(("turn", TURN_AT[n], 0))
        steps.append(tiles[0])
        if with_quad:
            steps.append(("scores", n, 0))
        steps.append(tiles[1])
        if with_quad:
            steps.append(("scores", n, 1))
        steps.append(tiles[2])
        if with_quad and n >= 1:
            steps.append(("values", n - 1, 0))
        steps.append(tiles[3])
        if with_quad and n in OUT_AT:
            steps += [(what, OUT_AT[n], 0) for what in out]
    if with_quad:
        steps.append(("values", NU - 1, 0))
    if with_max:
        steps.append(("turn", CHUNKS - 1, 0))
    if with_quad:
        steps += [(what, CHUNKS - 1, 0) for what in out]
    return [x for x in steps if x]


def ring(steps):
    turns = [x for x in steps if x[0] in ("max", "turn", "den", "out")]
    return {x: e for e, x in enumerate(turns)}


def ring_base(kind, q):
    if isinstance(q, int) and q < 0:
        return 0
    return len(ring(order(kind, False, True))) + q * len(ring(order(kind, True, True)))


def width(c, kt):
    o = max(0, kt - TPC * c) * P
    return CHUNK - o, o


def diagonals(n):
    return sum(1 for c, kt in UNITS[:n] if kt >= TPC * c)


def build(nc, x_in, wqkvT, woT, wk, bk, wv, bv, wf, bf, gateT, w1, b1, w2, b2, out):
    ctx = ExitStack()
    with ctx:
        def sb(name, shape, dt=F32):
            return ctx.enter_context(nc.sbuf_tensor(name, shape, dt))

        def sems(stage, names):
            return {n: ctx.enter_context(nc.semaphore(f"{stage}_{n}")) for n in names.split()}

        x = sb("x", [P, TILES, D])
        y = sb("y", [P, TILES, D])
        yT = sb("yT", [P, S])
        arena = sb("arena", [P, 4 * S * 2])
        probs_mem = sb("probs_mem", [P, 6144])
        v_quad = sb("v_quad", [P, TILES, QUAD * VW])
        v_all = sb("v_all", [P, TILES, HEADS * VW])
        o_tok = sb("o_tok", [P, TILES, HEADS * VW])
        w_qkv_sb = sb("w_qkv_sb", [P, 3 * D])
        w_out_sb = sb("w_out_sb", [P, QUADS, D])
        w_k_sb = sb("w_k_sb", [P, D])
        w1_sb = sb("w1_sb", [P, EXPERTS, HID])
        w2_sb = sb("w2_sb", [P, HCH, D])
        b1_sb = sb("b1_sb", [P, HCH])
        bk_sb = sb("bk_sb", [P, 1])
        bf_sb = sb("bf_sb", [P, D])
        b2_sum = sb("b2_sum", [P, 1, D])
        gate_sb = sb("gate_sb", [P, 2])
        gate_diff = sb("gate_diff", [P, D])
        ones = sb("ones", [P, P])
        ident = sb("ident", [P, P])
        by_width = sb("by_width", [P, P])
        ident_b = sb("ident_b", [P, P], BF16)
        above = sb("above", [P, P])
        stats = sb("stats", [P, TILES, 6])
        mean_var = sb("mean_var", [P, TILES, 2])
        deviation = sb("deviation", [P, TILES])
        rstd = sb("rstd", [P, TILES])
        max_parts = sb("max_parts", [P, QUAD, TPC, CHUNKS + 1])
        row_max = sb("row_max", [P, QUAD * TPC])
        max_rest = sb("max_rest", [P, QUAD * TPC])
        neg_max = sb("neg_max", [P, P // (QUAD * TPC), QUAD * TPC], BF16)
        max_rows = sb("max_rows", [PARTS * QUAD * TPC, CHUNKS, P], BF16)
        carry, act_word, dve_word = (sb(n, [1, 1]) for n in ("carry", "act_word", "dve_word"))
        masked_scores = sb("masked_scores", [P, 2, P])

        half = S * 2
        operands = [arena[:, i * half:(i + 1) * half].bitcast(BF16).rearrange("p (c h t) -> p c h t", c=CHUNKS, h=QUAD)
                    for i in range(4)]
        q_exp, q_max, k_exp, k_max = operands
        w_v_sb = arena[:, 3 * half:3 * half + HID]
        bv_sb = arena[:, 3 * half + HID:3 * half + 2 * HID]
        b2_sb = o_tok[:, 0, 0:3 * D].rearrange("p (e d) -> p e d", e=3)
        hidden = arena[:, 0:2 * HCH * CHUNK].rearrange("p (b m t) -> p b m t", b=2, m=HCH)
        probs = probs_mem[:, 0:4096].rearrange("p (b h t) -> p b h t", b=2, h=QUAD)
        parts = probs_mem[:, :].bitcast(BF16).rearrange("p (c w r t) -> p c w r t", c=CHUNKS, w=2, r=PARTS)
        rest = v_quad[:, :, :].rearrange("p t n -> p (t n)").rearrange("p (b w t) -> p b w t", b=2, w=2)
        masked = probs_mem[:, 0:2048].rearrange("p (b e t) -> p b e t", b=2, e=2)
        sums = yT[:, 0:2 * CHUNK].rearrange("p (w t) -> p w t", w=2)
        recip = sb("recip", [P, TPC, QUAD, 1])
        o_heads = o_tok[:, :, :].rearrange("p t (h d) -> p t h d", h=HEADS)
        o_narrow = o_tok[:, :, 0:D]
        turned_o = arena[:, 3 * half:4 * half].rearrange("p (b g t) -> p b g t", b=2, g=QUADS)
        x_c = [x[:, TPC * c:TPC * (c + 1), :] for c in range(CHUNKS)]
        y_c = [y[:, TPC * c:TPC * (c + 1), :] for c in range(CHUNKS)]

        psum = ctx.enter_context(nc.psum_tensor("psum", [P, 8, CHUNK], F32))
        bank = [psum[:, i, :] for i in range(8)]
        tiles_of = lambda b: b.rearrange("p (t d) -> p t d", t=TPC)
        SCORE, PV, DEN, RING = 0, 4, 5, 6

        scratch = {s: [nc.dram_tensor(f"rows_{s}_{w}", (ROWS, HEADS, S), BF16).ap() for w in "qk"]
                   for s in "ab"}
        x_dram = x_in.rearrange("(t p) d -> p t d", p=P)
        out_dram = out.rearrange("(t p) d -> p t d", p=P)

        load = sems("load", "x0 x1 x2 x3 w_qkv w_o w_f w_b w_ffn")
        const = sems("const", "zero ones ident above gate bias b2 v_ones")
        norm_names = "norm sqrt y turned yT "
        ffn = [sems(f"ffn{i}", norm_names + "gate masked up up_act up_dve down down_read x_bias out")
               for i in range(2)]
        att = {s: sems(f"att_{s}", norm_names +
                       "qk high rest mid low v v_stored rows0 rows1 rows2 rows3 pads x_plus "
                       "m0 m1 m2 m3 s0 s1 s2 s3 r0 r1 r2 r3 "
                       "scores exp kept pv ring_full ring_free cleared folded split "
                       "neg_max sums recip o o_back o_turned projected x_done") for s in "ab"}

        block = ctx.enter_context(nc.Block())

        def sync_rows(sp, kind):
            s = att[kind]
            for c in range(CHUNKS):
                tokens = slice(c * CHUNK, (c + 1) * CHUNK)
                sp.wait_ge(s["low"], 2 * (c + 1))
                sp.wait_ge(s["mid"], 2 * (c + 1))
                for w in range(2):
                    for part in range(PARTS):
                        blocks = [b for b, pair in enumerate(PAIRS) if pair[w] == part]
                        step = blocks[1] - blocks[0] if len(blocks) > 1 else 1
                        rows = scratch[kind][w].rearrange("(b d) h t -> (d h) b t", b=COMBOS)[
                            :, blocks[0]:blocks[-1] + 1:step, tokens]
                        source = parts[:, c, w, part:part + 1, :].to_broadcast([P, len(blocks), CHUNK])
                        sp.dma_start(rows, source).then_inc(s[f"rows{c}"], 16)

        def sync_quads(sp, kind):
            s = att[kind]
            rows_q, rows_k = scratch[kind]

            def piece(rows, quad, c):
                return rows[:, bass.ds(quad * QUAD, QUAD), c * CHUNK:(c + 1) * CHUNK]

            def load_max_q(quad, c):
                sp.dma_start(q_max[0:ROWS, c, :, :], piece(rows_q, quad, c)).then_inc(s[f"m{c}"], 16)

            def load_max_k(quad, c):
                sp.dma_start(k_max[0:ROWS, c, :, :], piece(rows_k, quad, c)).then_inc(s[f"m{c}"], 16)

            def load_exp_q(quad, c):
                sp.dma_start(q_exp[0:ROWS, c, :, :], piece(rows_q, quad, c)).then_inc(s[f"s{c}"], 16)

            def load_exp_kv(quad, c):
                sp.dma_start(k_exp[0:ROWS, c, :, :], piece(rows_k, quad, c)).then_inc(s[f"s{c}"], 16)
                sp.dma_start(v_quad[:, TPC * c:TPC * (c + 1), :],
                             v_all[:, TPC * c:TPC * (c + 1), bass.ds(quad * QUAD * VW, QUAD * VW)]).then_inc(s[f"s{c}"], 16)

            def place_rows(c):
                sp.dma_start(q_exp[ROWS:ROWS + PARTS, c, :, :].rearrange("p h (i t) -> p (h i) t", i=TPC),
                             max_rows[:, c, :]).then_inc(s[f"r{c}"], 16)

            sp.wait_ge(s["pads"], 8)
            for c in range(CHUNKS):
                sp.wait_ge(s[f"rows{c}"], 2 * PARTS * 16)
                load_max_q(0, c)
                load_max_k(0, c)
            sp.wait_ge(s["v_stored"], TILES if kind == "b" else CHUNKS)
            for c in range(CHUNKS):
                load_exp_q(0, c)
                load_exp_kv(0, c)

            def slot(q, with_quad, more):
                k = q + 1
                place = ring(order(kind, with_quad, True))
                base = ring_base(kind, q)

                def maxima_passed(units):
                    sp.wait_ge(s["ring_full"], base + place["max", units - 1, QUAD - 1] + 1)

                for c in range(CHUNKS):
                    if c == CHUNKS - 1:
                        for j in range(CHUNKS):
                            if with_quad:
                                sp.wait_ge(s["pv"], q * NU + FIRST[c] + TPC * (j + 1))
                                load_exp_kv(k, j)
                            if more:
                                maxima_passed(FIRST[c] + TPC * (j + 1))
                                load_max_k(q + 2, j)
                    if with_quad:
                        sp.wait_ge(s["pv"], q * NU + FIRST[c + 1])
                        load_exp_q(k, c)
                    if more:
                        maxima_passed(FIRST[c + 1])
                        load_max_q(q + 2, c)
                    sp.wait_ge(s["ring_free"], base + place["turn", c, 0] + 1)
                    place_rows(c)

            slot(-1, False, True)
            with sp.Fori(0, QUADS - 2) as q:
                slot(q, True, True)
            slot(QUADS - 2, True, False)

        @block.sync
        def _(sp):
            for c in range(CHUNKS):
                sp.dma_start(x_c[c], x_dram[:, TPC * c:TPC * (c + 1), :]).then_inc(load[f"x{c}"], 16)
            sp.dma_start(w_qkv_sb[:, :], wqkvT).then_inc(load["w_qkv"], 16)
            sp.dma_start(w_out_sb[:, 0, :], woT).then_inc(load["w_o"], 16)
            for dst, src in ((w_k_sb[:, :], wk), (bk_sb[:, :], bk), (bf_sb[:, :], bf.partition_broadcast(P))):
                sp.dma_start(dst, src).then_inc(load["w_b"], 16)
            sp.dma_start(w1_sb[:, :, :], w1.rearrange("e d h -> d e h")).then_inc(load["w_ffn"], 16)
            sp.dma_start(w2_sb[:, :, :], w2.rearrange("(m p) d -> p m d", p=P)).then_inc(load["w_ffn"], 16)
            sp.dma_start(b1_sb[:, :], b1).then_inc(load["w_ffn"], 16)
            sp.dma_start(gate_sb[:, :], gateT).then_inc(load["w_ffn"], 16)
            sp.dma_start(b2_sb[:, :, :], b2.partition_broadcast(P)).then_inc(load["w_ffn"], 16)
            sync_rows(sp, "a")
            sync_quads(sp, "a")
            sp.wait_ge(att["a"]["projected"], CHUNKS)
            sp.dma_start(w_v_sb, wv).then_inc(load["w_b"], 16)
            sp.dma_start(bv_sb, bv.partition_broadcast(P)).then_inc(load["w_b"], 16)
            sp.dma_start(w_out_sb[:, :, :], wf.rearrange("(g p) o -> p g o", p=P)).then_inc(load["w_f"], 16)
            sync_rows(sp, "b")
            sync_quads(sp, "b")
            for c in range(CHUNKS):
                sp.wait_ge(ffn[1]["out"], c + 1)
                sp.dma_start(out_dram[:, TPC * c:TPC * (c + 1), :], x_c[c]).then_inc(load["x0"], 16)
            sp.wait_ge(load["x0"], 16 * (1 + CHUNKS))

        LOAD_WEIGHTS_B = 5 * 16
        LOAD_WEIGHTS_FFN = 5 * 16
        TWO_BF16_ONES = float(np.array([0x3F803F80], np.uint32).view(np.float32)[0])

        def pool_pads(pool, kind):
            s = att[kind]
            for i, value in enumerate((0.0, 0.0, TWO_BF16_ONES, 0.0)):
                words = arena[:, i * half:(i + 1) * half]
                if i:
                    pool.wait_ge(s["pads"], 2 * i)
                pool.memset(words[32:64, :], value).then_inc(s["pads"], 1)
                pool.wait_ge(s["pads"], 2 * i + 1)
                pool.memset(words[64:128, :], value).then_inc(s["pads"], 1)
            pool.wait_ge(s["pads"], 8)

        def pool_low(pool, kind):
            s = att[kind]
            for c in range(CHUNKS):
                for w in range(2):
                    pool.wait_ge(s["mid"], 2 * c + w + 1)
                    pool.tensor_tensor(parts[:, c, w, 2, :], rest[:, c % 2, w, :], parts[:, c, w, 1, :],
                                       ALU.subtract).then_inc(s["low"], 1)

        def pool_quads(pool, kind):
            s = att[kind]

            def quad(q):
                for n, (c, kt) in enumerate(UNITS):
                    if kt >= TPC * c:
                        pool.wait_ge(s["exp"], q * 2 * NU + 2 * n + 2)
                        pool.wait_ge(s["kept"], q * diagonals(NU) + diagonals(n) + 1)
                        pool.tensor_tensor(carry[:, :], carry[:, :], carry[:, :], ALU.mult)
                        diagonal = probs[:, n % 2, :, 0:P]
                        pool.affine_select(out=diagonal, in_=diagonal, compare_op=ALU.is_ge, fill=0.0, base=0,
                                           pattern=[[0, QUAD], [1, P]], channel_multiplier=-1).then_inc(s["kept"], 1)

            pool.memset(carry[:, :], 0.0).then_inc(s["kept"], 1)
            with pool.Fori(0, QUADS) as q:
                quad(q)

        def pool_plus_bias(pool, i):
            s = ffn[i]
            for c in range(CHUNKS):
                pool.wait_ge(s["y"], TPC * (c + 1))
                pool.tensor_tensor(x_c[c], x_c[c], b2_sum[:, :, :].to_broadcast([P, TPC, D]),
                                   ALU.add).then_inc(s["x_bias"], 1)

        @block.gpsimd
        def _(pool):
            pool.memset(ones[:, :], 1.0).then_inc(const["ones"], 1)
            pool.memset(carry[:, :], 0.0)
            pool.memset(neg_max[:, :, :], 0.0).then_inc(const["zero"], 1)
            pool.memset(above[:, :], 0.0).then_inc(const["zero"], 1)
            pool.wait_ge(const["zero"], 2)
            pool.wait_ge(const["ones"], 1)
            pool.affine_select(out=ident[:, :], in_=ones[:, :], compare_op=ALU.is_equal, fill=0.0, base=0,
                               pattern=[[1, P]], channel_multiplier=-1).then_inc(const["ident"], 1)
            pool.affine_select(out=above[:, :], in_=above[:, :], compare_op=ALU.is_ge, fill=-3e38, base=0,
                               pattern=[[-1, P]], channel_multiplier=1).then_inc(const["above"], 1)
            pool.wait_ge(const["ident"], 1)
            pool.tensor_copy(ident_b[:, :], ident[:, :]).then_inc(const["ident"], 1)
            pool.tensor_copy(by_width[:, :].rearrange("p (d h) -> p d h", h=HEADS),
                             ident[:, :].rearrange("p (h d) -> p d h", h=HEADS)).then_inc(const["ident"], 1)
            pool.memset(v_all[:, :, :], 1.0).then_inc(const["v_ones"], 1)
            pool.wait_ge(const["v_ones"], 1)
            pool_pads(pool, "a")
            pool_low(pool, "a")
            pool.wait_ge(load["w_ffn"], LOAD_WEIGHTS_FFN)
            pool.tensor_tensor(b2_sum[:, 0, :], b2_sb[:, 0, :], b2_sb[:, 1, :], ALU.add).then_inc(const["b2"], 1)
            pool.wait_ge(const["b2"], 1)
            pool.tensor_tensor(b2_sum[:, 0, :], b2_sum[:, 0, :], b2_sb[:, 2, :], ALU.add).then_inc(const["b2"], 1)
            pool.tensor_tensor(gate_sb[:, 1:2], gate_sb[:, 1:2], gate_sb[:, 0:1], ALU.subtract).then_inc(const["gate"], 1)
            pool.wait_ge(const["gate"], 1)
            pool.tensor_scalar(gate_diff[:, :], ones[:, :], gate_sb[:, 1:2], None, ALU.mult).then_inc(const["gate"], 1)
            pool_quads(pool, "a")
            pool.wait_ge(const["b2"], 2)
            pool_plus_bias(pool, 0)
            pool_low(pool, "b")
            pool.wait_ge(ffn[0]["down"], CHUNKS)
            pool.wait_ge(att["b"]["v_stored"], TILES)
            pool.wait_ge(att["b"]["low"], 2 * CHUNKS)
            pool_pads(pool, "b")
            pool.wait_ge(load["w_b"], LOAD_WEIGHTS_B)
            for c in range(CHUNKS):
                pool.wait_ge(att["b"]["y"], TPC * (c + 1))
                pool.tensor_tensor(x_c[c], x_c[c], y_c[c], ALU.add).then_inc(att["b"]["x_plus"], 1)
                pool.wait_ge(att["b"]["x_plus"], 2 * c + 1)
                pool.tensor_tensor(x_c[c], x_c[c], bf_sb[:, :].rearrange("p (t d) -> p t d", t=1).to_broadcast([P, TPC, D]),
                                   ALU.add).then_inc(att["b"]["x_plus"], 1)
            pool_quads(pool, "b")
            pool_plus_bias(pool, 1)

        def pe_turn(pe, s, c, to):
            pe.wait_ge(s["y"], TPC * (c + 1))
            for t in range(TPC):
                last = nc.tensor.transpose(tiles_of(bank[to])[:, t, :], y[:, TPC * c + t, :], ident[:, :])
            last.then_inc(s["turned"], 1)

        def pe_project(pe, kind):
            s = att[kind]
            if kind == "a":
                pe.wait_ge(const["ident"], 1)
                pe.wait_ge(load["w_qkv"], 16)
            else:
                pe.wait_ge(load["w_b"], LOAD_WEIGHTS_B)
                pe.wait_ge(const["ident"], 3)
                pe.wait_ge(ffn[0]["out"], CHUNKS)
            for c in range(CHUNKS):
                if c >= 1:
                    pe.wait_ge(s["yT"], c)
                pe_turn(pe, s, c, 0)
                tokens = yT[:, c * CHUNK:(c + 1) * CHUNK]
                if c >= 1:
                    pe.wait_ge(s["rest"], 2 * c)
                pe.wait_ge(s["yT"], c + 1)
                if kind == "a":
                    nc.tensor.matmul(bank[2], w_qkv_sb[:, 0:D], tokens, start=True, stop=True).then_inc(s["qk"], 1)
                    nc.tensor.matmul(bank[3], w_qkv_sb[:, D:2 * D], tokens, start=True, stop=True).then_inc(s["qk"], 1)
                    if c >= 1:
                        pe.wait_ge(s["v_stored"], c)
                    for t in range(TPC):
                        last = nc.tensor.matmul(tiles_of(bank[4])[:, t, :], tokens[:, t * P:(t + 1) * P],
                                                w_qkv_sb[:, 2 * D:3 * D], start=True, stop=True)
                    last.then_inc(s["v"], 1)
                else:
                    nc.tensor.matmul(bank[2], by_width[:, :], tokens, start=True, stop=True).then_inc(s["qk"], 1)
                    nc.tensor.matmul(bank[3], w_k_sb[:, :], tokens, start=True, stop=True).then_inc(s["qk"], 1)
                    for t in range(TPC):
                        if c >= 1:
                            pe.wait_ge(s["v_stored"], TPC * (c - 1) + t + 1)
                        nc.tensor.matmul(bank[4 + t], tokens[:, t * P:(t + 1) * P], w_v_sb,
                                         start=True, stop=True).then_inc(s["v"], 1)

        def pe_quads(pe, kind):
            s = att[kind]

            def ring_turn(base, e):
                if not (isinstance(base, int) and base + e < 2):
                    pe.wait_ge(s["ring_free"], base + e - 1)

            def maxima(k, base, e, n, h):
                c, kc, i = COMBO[n]
                if n == FIRST[c] and h == 0:
                    pe.wait_ge(s[f"m{c}"], k * 32 + 32)
                w = CHUNK if kc < c else (i + 1) * P
                ring_turn(base, e)
                nc.tensor.matmul(bank[RING + e % 2][:, 0:w], q_max[:, c, h, i * P:(i + 1) * P],
                                 k_max[:, kc, h, 0:w], start=True, stop=True).then_inc(s["ring_full"], 1)

            def turn(k, base, e, c):
                pe.wait_ge(s["neg_max"], k * CHUNKS + c + 1)
                ring_turn(base, e)
                nc.tensor.transpose(bank[RING + e % 2].bitcast(BF16)[:, 0:P], neg_max[:, :, :].rearrange("p a b -> p (a b)"),
                                    ident_b[:, :]).then_inc(s["ring_full"], 1)

            def scores(q, n, pair):
                c, kt = UNITS[n]
                w, o = width(c, kt)
                if kt == 0 and pair == 0:
                    pe.wait_ge(s[f"s{c}"], q * 48 + 48)
                    pe.wait_ge(s[f"r{c}"], q * 16 + 16)
                if n >= 1:
                    pe.wait_ge(s["exp"], q * 2 * NU + 2 * (n - 1) + pair + 1)
                for h in (2 * pair, 2 * pair + 1):
                    last = nc.tensor.matmul(bank[SCORE + h][:, 0:w], k_exp[:, kt // TPC, h, kt % TPC * P:(kt % TPC + 1) * P],
                                            q_exp[:, c, h, o:CHUNK], start=True, stop=True)
                last.then_inc(s["scores"], 1)

            def values(q, n):
                c, kt = UNITS[n]
                w, o = width(c, kt)
                pe.wait_ge(s["exp"], q * 2 * NU + 2 * n + 2)
                if kt >= TPC * c:
                    pe.wait_ge(s["kept"], q * diagonals(NU) + diagonals(n) + 2)
                if kt == 0:
                    pe.wait_ge(s["sums"], q * CHUNKS + c + 1)
                ends = kt == TPC * (c + 1) - 1
                for h in range(QUAD):
                    last = nc.tensor.matmul(bank[PV][32 * h:32 * h + 32, o:CHUNK], v_quad[:, kt, VW * h:VW * (h + 1)],
                                            probs[:, n % 2, h, 0:w], start=kt == 0, stop=ends)
                if kind == "b":
                    for h in range(QUAD):
                        last = nc.tensor.matmul(bank[DEN][32 * h:32 * h + 32, o:CHUNK], ones[:, 0:VW],
                                                probs[:, n % 2, h, 0:w], start=kt == 0, stop=ends)
                last.then_inc(s["pv"], 1)

            def out_turn(q, base, e, c, which):
                pe.wait_ge(s["sums"], q * CHUNKS + c + 2)
                ring_turn(base, e)
                for t in range(TPC):
                    last = nc.tensor.transpose(tiles_of(bank[RING + e % 2])[:, t, :], sums[:, which, t * P:(t + 1) * P],
                                               ident[:, :])
                last.then_inc(s["ring_full"], 1)

            def slot(q, with_quad, with_max):
                steps = order(kind, with_quad, with_max)
                place = ring(steps)
                base = ring_base(kind, q)
                for step in steps:
                    what, n, h = step
                    if what == "max":
                        maxima(q + 1, base, place[step], n, h)
                    elif what == "turn":
                        turn(q + 1, base, place[step], n)
                    elif what == "scores":
                        scores(q, n, h)
                    elif what == "values":
                        values(q, n)
                    elif what == "den":
                        out_turn(q, base, place[step], n, 1)
                    else:
                        out_turn(q, base, place[step], n, 0)

            if kind == "a":
                pe.wait_ge(const["ident"], 2)
                pe.wait_ge(const["ones"], 1)
            pe.wait_ge(s["rest"], 2 * CHUNKS)
            pe.wait_ge(s["v_stored"], TILES if kind == "b" else CHUNKS)
            slot(-1, False, True)
            with pe.Fori(0, QUADS - 1) as q:
                slot(q, True, True)
            slot(QUADS - 1, True, False)

        def pe_out(pe, kind):
            s = att[kind]
            groups = 1 if kind == "a" else QUADS
            pe.wait_ge(load["w_o" if kind == "a" else "w_f"], 16)
            pe.wait_ge(s["o"], 1 + QUADS * CHUNKS)

            def turn_back(c):
                for g in range(groups):
                    if c >= 1:
                        pe.wait_ge(s["o_turned"], groups * (c - 1) + g + 1)
                    for t in range(TPC):
                        last = nc.tensor.transpose(tiles_of(bank[4 + g])[:, t, :],
                                                   o_tok[:, TPC * c + t, g * D:(g + 1) * D], ident[:, :])
                    last.then_inc(s["o_back"], 1)

            turn_back(0)
            for c in range(CHUNKS):
                if c < CHUNKS - 1:
                    turn_back(c + 1)
                pe.wait_ge(s["o_turned"], groups * (c + 1))
                for t in range(TPC):
                    for g in range(groups):
                        last = nc.tensor.matmul(tiles_of(bank[c])[:, t, :], turned_o[:, c % 2, g, t * P:(t + 1) * P],
                                                w_out_sb[:, g, :], start=g == 0, stop=g == groups - 1)
                last.then_inc(s["projected"], 1)

        def pe_ffn(pe, i):
            s = ffn[i]
            pe.wait_ge(load["w_ffn"], LOAD_WEIGHTS_FFN)
            pe.wait_ge(const["gate"], 2)
            before = att["ab"[i]]
            pe.wait_ge(before["x_done"], CHUNKS)

            def turn_and_gate(c):
                pe_turn(pe, s, c, 0)
                pe.wait_ge(s["yT"], c + 1)
                nc.tensor.matmul(bank[1], gate_diff[:, :], yT[:, c * CHUNK:(c + 1) * CHUNK],
                                 start=True, stop=True).then_inc(s["gate"], 1)

            turn_and_gate(0)
            for c in range(CHUNKS):
                for m in range(HCH):
                    e, j = divmod(m, HID // P)
                    u = c * HCH + m
                    if u >= 4:
                        pe.wait_ge(s["up_act" if u % 2 == 0 else "up_dve"], (u - 4) // 2 + 1)
                    if m == HID // P:
                        pe.wait_ge(s["masked"], 2 * (c + 1))
                    if e == 0:
                        tokens = yT[:, c * CHUNK:(c + 1) * CHUNK]
                    else:
                        tokens = masked[:, c % 2, e - 1, :]
                    nc.tensor.matmul(bank[4 + u % 4], w1_sb[:, e, j * P:(j + 1) * P], tokens,
                                     start=True, stop=True).then_inc(s["up"], 1)
                if c < CHUNKS - 1:
                    turn_and_gate(c + 1)
                pe.wait_ge(s["up_act"], HCH // 2 * (c + 1))
                pe.wait_ge(s["up_dve"], HCH // 2 * (c + 1))
                if c >= 2:
                    pe.wait_ge(s["out"], c - 1)
                for t in range(TPC):
                    for m in range(HCH):
                        last = nc.tensor.matmul(tiles_of(bank[2 + c % 2])[:, t, :], hidden[:, c % 2, m, t * P:(t + 1) * P],
                                                w2_sb[:, m, :], start=m == 0, stop=m == HCH - 1)
                last.then_inc(s["down"], 1)

        @block.tensor
        def _(pe):
            pe_project(pe, "a")
            pe_quads(pe, "a")
            pe_out(pe, "a")
            pe_ffn(pe, 0)
            pe_project(pe, "b")
            pe_quads(pe, "b")
            pe_out(pe, "b")
            pe_ffn(pe, 1)

        def act_sqrt(act, s):
            act.wait_ge(s["norm"], 2 * TILES + 1)
            nc.scalar.activation(deviation[:, :], rstd[:, :], ACT.Sqrt).then_inc(s["sqrt"], 1)

        def act_store_yT(act, s, c):
            act.wait_ge(s["turned"], c + 1)
            nc.scalar.copy(yT[:, c * CHUNK:(c + 1) * CHUNK], bank[0]).then_inc(s["yT"], 1)

        def act_project(act, kind):
            s = att[kind]
            act_sqrt(act, s)
            v_heads = v_all[:, :, :].rearrange("p t (h w) -> p t h w", h=HEADS)

            def high(c, w):
                act.wait_ge(s["qk"], 2 * c + w + 1)
                source = bank[2 + w]
                if kind == "b" and w == 1:
                    nc.scalar.activation(parts[:, c, w, 0, :], source, ACT.Identity, bias=bk_sb[:, 0:1]).then_inc(s["high"], 1)
                else:
                    nc.scalar.copy(parts[:, c, w, 0, :], source).then_inc(s["high"], 1)

            for c in range(CHUNKS):
                act_store_yT(act, s, c)
                high(c, 0)
                high(c, 1)
                if kind == "a":
                    if c == 0:
                        act.wait_ge(const["v_ones"], 1)
                    act.wait_ge(s["v"], c + 1)
                    nc.scalar.copy(v_heads[:, TPC * c:TPC * (c + 1), :, 0:HD],
                                   bank[4].rearrange("p (t h d) -> p t h d", t=TPC, h=HEADS)).then_inc(s["v_stored"], 1)
                for w in range(2):
                    act.wait_ge(s["rest"], 2 * c + w + 1)
                    nc.scalar.copy(parts[:, c, w, 1, :], rest[:, c % 2, w, :]).then_inc(s["mid"], 1)

        def act_quads(act, kind):
            s = att[kind]
            scale = HD ** -0.5 if kind == "a" else 1.0

            def copy_sums(q, c):
                act.wait_ge(s["pv"], q * NU + FIRST[c + 1])
                act.wait_ge(s["o"], q * CHUNKS + c + 1)
                banks = 1 if kind == "a" else 2
                nc.scalar.copy(sums[:, 0:banks, :], psum[:, PV:PV + banks, :]).then_inc(s["sums"], 1)

            def quad(q):
                for n, (c, kt) in enumerate(UNITS):
                    w, o = width(c, kt)
                    for pair in range(2):
                        act.wait_ge(s["scores"], q * 2 * NU + 2 * n + pair + 1)
                        if n >= 2 and pair == 0:
                            act.wait_ge(s["pv"], q * NU + n - 1)
                        heads = slice(2 * pair, 2 * pair + 2)
                        nc.scalar.activation(probs[:, n % 2, heads, 0:w], psum[:, SCORE + 2 * pair:SCORE + 2 * pair + 2, 0:w],
                                             ACT.Exp, scale=scale).then_inc(s["exp"], 1)
                    if n in FIRST[1:]:
                        copy_sums(q, FIRST.index(n) - 1)
                copy_sums(q, CHUNKS - 1)

            nc.scalar.copy(act_word[:, :], ones[0:1, 0:1]).then_inc(s["sums"], 1)
            act.wait_ge(s["low"], 2 * CHUNKS)
            for c in range(CHUNKS):
                act.wait_ge(s[f"rows{c}"], 2 * PARTS * 16)
            with act.Fori(0, QUADS) as q:
                quad(q)

        def act_out(act, kind):
            s = att[kind]
            groups = 1 if kind == "a" else QUADS
            for c in range(CHUNKS):
                for g in range(groups):
                    act.wait_ge(s["o_back"], groups * c + g + 1)
                    if c >= 2 and g == 0:
                        act.wait_ge(s["projected"], c - 1)
                    nc.scalar.activation(turned_o[:, c % 2, g, :], bank[4 + g],
                                         ACT.Gelu if kind == "b" else ACT.Copy).then_inc(s["o_turned"], 1)

        def act_ffn(act, i):
            s = ffn[i]
            act_sqrt(act, s)
            act_store_yT(act, s, 0)
            for c in range(CHUNKS):
                if c >= 2:
                    act.wait_ge(s["down"], c - 1)
                for m in range(0, HCH, 2):
                    u = c * HCH + m
                    act.wait_ge(s["up"], u + 1)
                    nc.scalar.activation(hidden[:, c % 2, m, :], bank[4 + u % 4], ACT.Relu,
                                         bias=b1_sb[:, m:m + 1]).then_inc(s["up_act"], 1)
                if c < CHUNKS - 1:
                    act_store_yT(act, s, c + 1)

        @block.scalar
        def _(act):
            act_project(act, "a")
            act_quads(act, "a")
            act_out(act, "a")
            act_ffn(act, 0)
            act_project(act, "b")
            act_quads(act, "b")
            act_out(act, "b")
            act_ffn(act, 1)

        def dve_norm(dve, s, ready):
            for t in range(TILES):
                if t % TPC == 0:
                    ready(t // TPC)
                nc.vector.bn_stats(stats[:, t, :], x[:, t, :]).then_inc(s["norm"], 1)
            for t in range(TILES):
                dve.wait_ge(s["norm"], t + 1)
                nc.vector.bn_aggr(mean_var[:, t, :], stats[:, t, :]).then_inc(s["norm"], 1)
            dve.wait_ge(s["norm"], 2 * TILES)
            nc.vector.tensor_scalar(rstd[:, :], mean_var[:, :, 1], EPS, None, ALU.add).then_inc(s["norm"], 1)
            dve.wait_ge(s["sqrt"], 1)
            nc.vector.reciprocal(rstd[:, :], deviation[:, :]).then_inc(s["norm"], 1)
            dve.wait_ge(s["norm"], 2 * TILES + 2)
            for t in range(TILES):
                nc.vector.tensor_scalar(y[:, t, :], x[:, t, :], mean_var[:, t, 0:1], rstd[:, t:t + 1],
                                        ALU.subtract, ALU.mult).then_inc(s["y"], 1)

        def dve_project(dve, kind):
            s = att[kind]
            for c in range(CHUNKS):
                for w in range(2):
                    dve.wait_ge(s["high"], 2 * c + w + 1)
                    if c >= 2:
                        dve.wait_ge(s["low"], 2 * (c - 2) + w + 1)
                    if kind == "b" and w == 1:
                        nc.vector.scalar_tensor_tensor(rest[:, c % 2, w, :], bank[3], bk_sb[:, 0:1], parts[:, c, w, 0, :],
                                                       ALU.add, ALU.subtract).then_inc(s["rest"], 1)
                    else:
                        nc.vector.tensor_tensor(rest[:, c % 2, w, :], bank[2 + w], parts[:, c, w, 0, :],
                                                ALU.subtract).then_inc(s["rest"], 1)
                if kind == "b":
                    for t in range(TPC):
                        dve.wait_ge(s["v"], TPC * c + t + 1)
                        nc.vector.tensor_tensor(v_all[:, TPC * c + t, :], bank[4 + t], bv_sb, ALU.add
                                                ).then_inc(s["v_stored"], 1)

        def dve_quads(dve, kind):
            s = att[kind]

            def maxima(k, base, e, n, h):
                c, kc, i = COMBO[n]
                if n == FIRST[c] and h == 0:
                    if not (isinstance(k, int) and k == 0 and c == 0):
                        dve.wait_ge(s["folded"], k * CHUNKS + c)
                    nc.vector.memset(max_parts[:, :, :, :], -3e38).then_inc(s["cleared"], 1)
                    dve.wait_ge(s["cleared"], k * CHUNKS + c + 1)
                scores = bank[RING + e % 2]
                w = CHUNK if kc < c else i * P
                if kc == c and not (isinstance(base, int) and base + e < 2):
                    dve.wait_ge(s["ring_free"], base + e - 1)
                dve.wait_ge(s["ring_full"], base + e + 1)
                if w:
                    last = nc.vector.tensor_reduce(max_parts[:, h, i, kc:kc + 1], scores[:, 0:w], AX.X, ALU.max)
                else:
                    nc.vector.memset(max_parts[:, h, i, kc:kc + 1], -3e38)
                if kc == c:
                    last = nc.vector.tensor_tensor_reduce(masked_scores[:, e % 2, :], scores[:, w:w + P], above[:, :], 1.0, -3e38,
                                                          ALU.add, ALU.max, max_parts[:, h, i, CHUNKS:CHUNKS + 1])
                last.then_inc(s["ring_free"], 1)
                if n + 1 in FIRST and h == QUAD - 1:
                    fold(k, c, base + e + 1)

            def fold(k, c, entries):
                dve.wait_ge(s["ring_free"], entries)
                nc.vector.tensor_reduce(row_max[:, :].rearrange("p (h i) -> p h i", h=QUAD), max_parts[:, :, :, :],
                                        AX.X, ALU.max).then_inc(s["folded"], 1)
                dve.wait_ge(s["folded"], k * CHUNKS + c + 1)
                nc.vector.tensor_scalar(neg_max[:, 0, :], row_max[:, :], -1.0, None, ALU.mult).then_inc(s["split"], 1)
                dve.wait_ge(s["split"], (k * CHUNKS + c) * 3 + 1)
                nc.vector.scalar_tensor_tensor(max_rest[:, :], row_max[:, :], -1.0, neg_max[:, 0, :],
                                               ALU.mult, ALU.subtract).then_inc(s["split"], 1)
                dve.wait_ge(s["split"], (k * CHUNKS + c) * 3 + 2)
                nc.vector.tensor_copy(neg_max[:, 1, :], max_rest[:, :]).then_inc(s["split"], 1)
                dve.wait_ge(s["split"], (k * CHUNKS + c) * 3 + 3)
                nc.vector.tensor_tensor(neg_max[:, 2, :], max_rest[:, :], neg_max[:, 1, :], ALU.subtract).then_inc(s["neg_max"], 1)

            def turn(k, base, e, c):
                dve.wait_ge(s["ring_full"], base + e + 1)
                if not (isinstance(k, int) and k == 0):
                    dve.wait_ge(s[f"r{c}"], k * 16)
                nc.vector.tensor_copy(max_rows[:, c, :], bank[RING + e % 2].bitcast(BF16)[0:PARTS * QUAD * TPC, 0:P]
                                      ).then_inc(s["ring_free"], 1)

            def denominators(q, base, e, c):
                dve.wait_ge(s["ring_full"], base + e + 1)
                dve.wait_ge(s["o"], q * CHUNKS + c + 1)
                column = HD if kind == "a" else 0
                inverse = nc.vector.reciprocal(recip[:, :, :, :], bank[RING + e % 2].rearrange(
                    "p (t h d) -> p t h d", t=TPC, h=QUAD)[:, :, :, column:column + 1])
                if kind == "a":
                    inverse.then_inc(s["recip"], 1)
                else:
                    inverse.then_inc(s["ring_free"], 1)

            def normalise(q, base, e, c):
                wide = HD if kind == "a" else VW
                if kind == "a":
                    denominators(q, base, e, c)
                    dve.wait_ge(s["recip"], q * CHUNKS + c + 1)
                else:
                    dve.wait_ge(s["ring_full"], base + e + 1)
                    dve.wait_ge(s["ring_free"], base + e)
                values = bank[RING + e % 2].rearrange("p (t h d) -> p t h d", t=TPC, h=QUAD)[:, :, :, 0:wide]
                o = o_tok[:, TPC * c:TPC * (c + 1), bass.ds(q * QUAD * wide, QUAD * wide)]
                nc.vector.tensor_tensor(o.rearrange("p t (h d) -> p t h d", h=QUAD), values,
                                        recip[:, :, :, :].to_broadcast([P, TPC, QUAD, wide]), ALU.mult).then_inc(s["o"], 1)
                dve.wait_ge(s["o"], q * CHUNKS + c + 2)
                nc.vector.memset(dve_word[:, :], 0.0).then_inc(s["ring_free"], 1)

            def slot(q, with_quad, with_max):
                place = ring(order(kind, with_quad, with_max))
                base = ring_base(kind, q)
                for step, e in place.items():
                    what, n, h = step
                    if what == "max":
                        maxima(q + 1, base, e, n, h)
                    elif what == "turn":
                        turn(q + 1, base, e, n)
                    elif what == "den":
                        denominators(q, base, e, n)
                    else:
                        normalise(q, base, e, n)

            if kind == "a":
                dve.wait_ge(const["above"], 1)
                dve.wait_ge(const["b2"], 2)
            nc.vector.memset(dve_word[:, :], 0.0).then_inc(s["o"], 1)
            slot(-1, False, True)
            with dve.Fori(0, QUADS - 1) as q:
                slot(q, True, True)
            slot(QUADS - 1, True, False)

        def dve_add(dve, s, c, done, count, source):
            dve.wait_ge(s[done], count)
            return nc.vector.tensor_tensor(x_c[c], tiles_of(source), x_c[c], ALU.add)

        def dve_ffn(dve, i):
            s = ffn[i]
            before = att["ab"[i]]
            dve_norm(dve, s, lambda c: dve.wait_ge(before["x_done"], c + 1))

            def mask(c):
                dve.wait_ge(s["gate"], c + 1)
                tokens = yT[:, c * CHUNK:(c + 1) * CHUNK]
                for e, chooses in enumerate((ALU.is_le, ALU.is_gt)):
                    nc.vector.scalar_tensor_tensor(masked[:, c % 2, e, :], bank[1], 0.0, tokens,
                                                   chooses, ALU.mult).then_inc(s["masked"], 1)

            mask(0)
            for c in range(CHUNKS):
                if c >= 2:
                    dve.wait_ge(s["down"], c - 1)
                for m in range(1, HCH, 2):
                    u = c * HCH + m
                    dve.wait_ge(s["up"], u + 1)
                    nc.vector.tensor_scalar(hidden[:, c % 2, m, :], bank[4 + u % 4], b1_sb[:, m:m + 1], 0.0,
                                            ALU.add, ALU.max).then_inc(s["up_dve"], 1)
                if c < CHUNKS - 1:
                    mask(c + 1)
                dve.wait_ge(s["x_bias"], c + 1)
                dve_add(dve, s, c, "down", c + 1, bank[2 + c % 2]).then_inc(s["out"], 1)

        @block.vector
        def _(dve):
            dve_norm(dve, att["a"], lambda c: dve.wait_ge(load[f"x{c}"], 16))
            dve_project(dve, "a")
            dve_quads(dve, "a")
            for c in range(CHUNKS):
                dve_add(dve, att["a"], c, "projected", c + 1, bank[c]).then_inc(att["a"]["x_done"], 1)
            dve_ffn(dve, 0)
            dve_norm(dve, att["b"], lambda c: dve.wait_ge(ffn[0]["out"], c + 1))
            dve_project(dve, "b")
            dve_quads(dve, "b")
            dve.wait_ge(att["b"]["x_plus"], 2 * CHUNKS)
            for c in range(CHUNKS):
                dve_add(dve, att["b"], c, "projected", c + 1, bank[c]).then_inc(att["b"]["x_done"], 1)
            dve_ffn(dve, 1)


def kernel(**inputs):
    from concourse import bacc
    from concourse.bass_utils import run_bass_kernel_spmd

    a = {k: np.ascontiguousarray(v) for k, v in inputs.items()}

    def by_width(w):
        return w.reshape(w.shape[0], HEADS, HD).transpose(0, 2, 1).reshape(w.shape)

    w_qkv = a["L0_attn_a_w_qkv"].T
    arrays = {
        "x_in": a["L0_attn_a_x"].reshape(S, D),
        "wqkvT": np.concatenate([by_width(w_qkv[:, :D]), by_width(w_qkv[:, D:2 * D]), w_qkv[:, 2 * D:]], 1),
        "woT": a["L0_attn_a_w_out"].T,
        "wk": by_width(a["L0_attn_b_Wk"]),
        "bk": by_width(a["L0_attn_b_bk"].reshape(1, D)).T,
        "wv": a["L0_attn_b_Wv"],
        "bv": a["L0_attn_b_bv"],
        "wf": a["L0_attn_b_Wf"],
        "bf": a["L0_attn_b_bf"],
        "gateT": a["L0_ffn_gate_w"].T,
        "w1": np.concatenate([a["L0_ffn_sw1"][None], a["L0_ffn_w1"]]),
        "b1": np.concatenate([a["L0_ffn_sb1"][None], a["L0_ffn_b1"]]).reshape(HCH, P).T,
        "w2": np.concatenate([a["L0_ffn_sw2"], a["L0_ffn_w2"].reshape(-1, D)]),
        "b2": np.concatenate([a["L0_ffn_sb2"][None], a["L0_ffn_b2"]]),
    }
    nc = bacc.Bacc("TRN2", target_bir_lowering=False, num_devices=1)
    maps, args = {}, []
    for name, array in arrays.items():
        array = np.ascontiguousarray(array)
        maps[f"in_{name}"] = array
        args.append(nc.dram_tensor(f"in_{name}", array.shape, mybir.dt.from_np(array.dtype), kind="ExternalInput").ap())
    out = nc.dram_tensor("out_x", (S, D), F32, kind="ExternalOutput").ap()
    build(nc, *args, out)
    result = run_bass_kernel_spmd(nc, [maps], core_ids=[0])
    return result.results[0]["out_x"].reshape(1, S, D)
```

```python
from contextlib import ExitStack

import concourse.bass as bass
import numpy as np
from concourse import mybir

F32 = mybir.dt.float32
BF16 = mybir.dt.bfloat16
ALU = mybir.AluOpType
ACT = mybir.ActivationFunctionType
AX = mybir.AxisListType

P = 128
S = 2048
D = 128
HEADS = 16
HD = D // HEADS
QUAD = 4
QUADS = HEADS // QUAD
TILES = S // P
CHUNK = 512
CHUNKS = S // CHUNK
TPC = CHUNK // P
VW = 32
HID = 512
EXPERTS = 3
HCH = EXPERTS * HID // P
EPS = 1e-5

PAIRS = [(0, 2), (0, 1), (0, 0), (1, 0), (2, 0), (1, 1)]
COMBOS = len(PAIRS)
ROWS = COMBOS * HD
PARTS = 3

UNITS = [(c, kt) for c in range(CHUNKS) for kt in range(TPC * (c + 1))]
NU = len(UNITS)
FIRST = [UNITS.index((c, 0)) for c in range(CHUNKS)] + [NU]
COMBO = [(c, kc, i) for c in range(CHUNKS) for kc in range(c + 1) for i in range(TPC)]
LEAD = 20
TURN_LAG, OUT_LAG = 1, 2
OPENING, MIDDLE, CLOSING = range(3)


def order(kind, stretch):
    exps = stretch != OPENING
    out = ("out",) if kind == "a" else ("den", "out")
    steps = []
    for n in range(LEAD if stretch == OPENING else 0, NU):
        ahead, m = divmod(n + LEAD, NU)
        for late in (0, 1):
            for c in range(CHUNKS):
                if n + LEAD == FIRST[c + 1] + TURN_LAG + late * NU and (stretch == MIDDLE or late == (stretch == OPENING)):
                    steps.append(("turn", late, c, 0))
        with_max = stretch == MIDDLE or ahead == (stretch == OPENING)
        tiles = [("max", ahead, m, h) if with_max else None for h in range(QUAD)]
        steps.append(tiles[0])
        if exps:
            steps.append(("scores", 0, n, 0))
        steps.append(tiles[1])
        if exps:
            steps.append(("scores", 0, n, 1))
        steps.append(tiles[2])
        if exps and n >= 1:
            steps.append(("values", 0, n - 1, 0))
        steps.append(tiles[3])
        if exps and n - OUT_LAG in FIRST[1:]:
            steps += [(what, 0, FIRST.index(n - OUT_LAG) - 1, 0) for what in out]
    if exps:
        steps.append(("values", 0, NU - 1, 0))
        steps += [(what, 0, CHUNKS - 1, 0) for what in out]
    return [x for x in steps if x]


def ring(kind, stretch):
    turns = [x for x in order(kind, stretch) if x[0] in ("max", "turn", "den", "out")]
    return {x: e for e, x in enumerate(turns)}


def ring_base(kind, stretch, q):
    if stretch == OPENING:
        return 0
    return len(ring(kind, OPENING)) + q * len(ring(kind, MIDDLE))


def width(c, kt):
    o = max(0, kt - TPC * c) * P
    return CHUNK - o, o


def diagonals(n):
    return sum(1 for c, kt in UNITS[:n] if kt >= TPC * c)


def build(nc, x_in, wqkvT, woT, wk, bk, wv, bv, wf, bf, gateT, w1, b1, w2, b2, out):
    ctx = ExitStack()
    with ctx:
        def sb(name, shape, dt=F32):
            return ctx.enter_context(nc.sbuf_tensor(name, shape, dt))

        def sems(stage, names):
            return {n: ctx.enter_context(nc.semaphore(f"{stage}_{n}")) for n in names.split()}

        x = sb("x", [P, TILES, D])
        y = sb("y", [P, TILES, D])
        yT = sb("yT", [P, S])
        arena = sb("arena", [P, 4 * S * 2])
        probs_mem = sb("probs_mem", [P, 6144])
        v_quad = sb("v_quad", [P, TILES, QUAD * VW])
        v_all = sb("v_all", [P, TILES, HEADS * VW])
        o_tok = sb("o_tok", [P, TILES, HEADS * VW])
        w_qkv_sb = sb("w_qkv_sb", [P, 3 * D])
        w_out_sb = sb("w_out_sb", [P, QUADS, D])
        w_k_sb = sb("w_k_sb", [P, D])
        w1_sb = sb("w1_sb", [P, EXPERTS, HID])
        w2_sb = sb("w2_sb", [P, HCH, D])
        b1_sb = sb("b1_sb", [P, HCH])
        bk_sb = sb("bk_sb", [P, 1])
        bf_sb = sb("bf_sb", [P, D])
        b2_sum = sb("b2_sum", [P, 1, D])
        gate_sb = sb("gate_sb", [P, 2])
        gate_diff = sb("gate_diff", [P, D])
        ones = sb("ones", [P, P])
        ident = sb("ident", [P, P])
        by_width = sb("by_width", [P, P])
        ident_b = sb("ident_b", [P, P], BF16)
        above = sb("above", [P, P], BF16)
        stats = sb("stats", [P, TILES, 6])
        mean_var = sb("mean_var", [P, TILES, 2])
        deviation = sb("deviation", [P, TILES])
        rstd = sb("rstd", [P, TILES])
        max_parts = sb("max_parts", [P, QUAD, TPC, CHUNKS])
        row_max = sb("row_max", [P, QUAD * TPC])
        max_rest = sb("max_rest", [P, QUAD * TPC])
        neg_max = sb("neg_max", [P, P // (QUAD * TPC), QUAD * TPC], BF16)
        max_rows = sb("max_rows", [PARTS * QUAD * TPC, CHUNKS, P], BF16)
        carry, act_word, dve_word = (sb(n, [1, 1]) for n in ("carry", "act_word", "dve_word"))

        half = S * 2
        operands = [arena[:, i * half:(i + 1) * half].bitcast(BF16).rearrange("p (c h t) -> p c h t", c=CHUNKS, h=QUAD)
                    for i in range(4)]
        q_exp, q_max, k_exp, k_max = operands
        w_v_sb = arena[:, 3 * half:3 * half + HID]
        bv_sb = arena[:, 3 * half + HID:3 * half + 2 * HID]
        b2_sb = o_tok[:, 0, 0:3 * D].rearrange("p (e d) -> p e d", e=3)
        hidden = arena[:, 0:2 * HCH * CHUNK].rearrange("p (b m t) -> p b m t", b=2, m=HCH)
        probs = probs_mem[:, 0:4096].rearrange("p (b h t) -> p b h t", b=2, h=QUAD)
        parts = probs_mem[:, :].bitcast(BF16).rearrange("p (c w r t) -> p c w r t", c=CHUNKS, w=2, r=PARTS)
        rest = v_quad[:, :, :].rearrange("p t n -> p (t n)").rearrange("p (b w t) -> p b w t", b=2, w=2)
        masked = probs_mem[:, 0:2048].rearrange("p (b e t) -> p b e t", b=2, e=2)
        sums = yT[:, 0:2 * CHUNK].rearrange("p (w t) -> p w t", w=2)
        recip = sb("recip", [P, TPC, QUAD, 1])
        o_heads = o_tok[:, :, :].rearrange("p t (h d) -> p t h d", h=HEADS)
        o_narrow = o_tok[:, :, 0:D]
        turned_o = arena[:, 3 * half:4 * half].rearrange("p (b g t) -> p b g t", b=2, g=QUADS)
        x_c = [x[:, TPC * c:TPC * (c + 1), :] for c in range(CHUNKS)]
        y_c = [y[:, TPC * c:TPC * (c + 1), :] for c in range(CHUNKS)]

        psum = ctx.enter_context(nc.psum_tensor("psum", [P, 8, CHUNK], F32))
        bank = [psum[:, i, :] for i in range(8)]
        tiles_of = lambda b: b.rearrange("p (t d) -> p t d", t=TPC)
        SCORE, PV, DEN = 0, 4, 5
        RING = {"a": 5, "b": 6}

        def ring_bank(kind, stretch, e):
            size = 8 - RING[kind]
            assert len(ring(kind, MIDDLE)) % size == 0
            return bank[RING[kind] + (ring_base(kind, stretch, 0) + e) % size]

        def early(stretch, e, turns):
            return stretch == OPENING and e < turns

        scratch = {s: [nc.dram_tensor(f"rows_{s}_{w}", (ROWS, HEADS, S), BF16).ap() for w in "qk"]
                   for s in "ab"}
        x_dram = x_in.rearrange("(t p) d -> p t d", p=P)
        out_dram = out.rearrange("(t p) d -> p t d", p=P)

        load = sems("load", "x0 x1 x2 x3 w_qkv w_o w_f w_b w_ffn")
        const = sems("const", "zero ones ident above gate bias b2 v_ones")
        norm_names = "norm sqrt y turned yT "
        ffn = [sems(f"ffn{i}", norm_names + "gate masked up up_act up_dve down down_read x_bias out")
               for i in range(2)]
        att = {s: sems(f"att_{s}", norm_names +
                       "qk high rest mid low v v_stored rows0 rows1 rows2 rows3 pads x_plus "
                       "m0 m1 m2 m3 s0 s1 s2 s3 r0 r1 r2 r3 "
                       "scores exp kept pv ring_full ring_free cleared folded split "
                       "neg_max sums recip o o_back o_turned projected x_done") for s in "ab"}

        block = ctx.enter_context(nc.Block())

        def sync_rows(sp, kind):
            s = att[kind]
            for c in range(CHUNKS):
                tokens = slice(c * CHUNK, (c + 1) * CHUNK)
                sp.wait_ge(s["low"], 2 * (c + 1))
                sp.wait_ge(s["mid"], 2 * (c + 1))
                for w in range(2):
                    for part in range(PARTS):
                        blocks = [b for b, pair in enumerate(PAIRS) if pair[w] == part]
                        step = blocks[1] - blocks[0] if len(blocks) > 1 else 1
                        rows = scratch[kind][w].rearrange("(b d) h t -> (d h) b t", b=COMBOS)[
                            :, blocks[0]:blocks[-1] + 1:step, tokens]
                        source = parts[:, c, w, part:part + 1, :].to_broadcast([P, len(blocks), CHUNK])
                        sp.dma_start(rows, source).then_inc(s[f"rows{c}"], 16)

        def sync_quads(sp, kind):
            s = att[kind]
            rows_q, rows_k = scratch[kind]

            def piece(rows, quad, c):
                return rows[:, bass.ds(quad * QUAD, QUAD), c * CHUNK:(c + 1) * CHUNK]

            def load_max_q(quad, c):
                sp.dma_start(q_max[0:ROWS, c, :, :], piece(rows_q, quad, c)).then_inc(s[f"m{c}"], 16)

            def load_max_k(quad, c):
                sp.dma_start(k_max[0:ROWS, c, :, :], piece(rows_k, quad, c)).then_inc(s[f"m{c}"], 16)

            def load_exp_q(quad, c):
                sp.dma_start(q_exp[0:ROWS, c, :, :], piece(rows_q, quad, c)).then_inc(s[f"s{c}"], 16)

            def load_exp_kv(quad, c):
                sp.dma_start(v_quad[:, TPC * c:TPC * (c + 1), :],
                             v_all[:, TPC * c:TPC * (c + 1), bass.ds(quad * QUAD * VW, QUAD * VW)]).then_inc(s[f"s{c}"], 16)
                sp.dma_start(k_exp[0:ROWS, c, :, :], piece(rows_k, quad, c)).then_inc(s[f"s{c}"], 16)

            def place_rows(c):
                sp.dma_start(q_exp[ROWS:ROWS + PARTS, c, :, :].rearrange("p h (i t) -> p (h i) t", i=TPC),
                             max_rows[:, c, :]).then_inc(s[f"r{c}"], 16)

            sp.wait_ge(s["pads"], 8)
            for c in range(CHUNKS):
                sp.wait_ge(s[f"rows{c}"], 2 * PARTS * 16)
                load_max_q(0, c)
                load_max_k(0, c)
            sp.wait_ge(s["v_stored"], TILES if kind == "b" else CHUNKS)
            for c in range(CHUNKS):
                load_exp_q(0, c)
                load_exp_kv(0, c)

            def slot(stretch, q, next_exp, next_max):
                place = ring(kind, stretch)
                base = ring_base(kind, stretch, q)
                for n in range(LEAD if stretch == OPENING else 0, NU):
                    ahead, m = divmod(n + LEAD, NU)
                    c, kc, i = COMBO[m]
                    if ("max", ahead, m, 0) in place and next_max[ahead] and i == TPC - 1:
                        if kc == c or (c == CHUNKS - 1 and kc > 0):
                            sp.wait_ge(s["ring_full"], base + place["max", ahead, m, QUAD - 1] + 1)
                        if c == CHUNKS - 1 and kc > 0:
                            load_max_k(q + ahead + 1, kc)
                        if c == CHUNKS - 1 and kc == 1:
                            load_max_k(q + ahead + 1, 0)
                        if kc == c:
                            load_max_q(q + ahead + 1, c)
                    if next_exp and n >= 1:
                        c, kt = UNITS[n - 1]
                        if c == CHUNKS - 1 and kt % TPC == TPC - 1:
                            sp.wait_ge(s["pv"], q * NU + n)
                            load_exp_kv(q + 1, kt // TPC)
                            load_exp_q(q + 1, kt // TPC)
                    for what, late, c, _ in place:
                        if what == "turn" and n + LEAD == FIRST[c + 1] + TURN_LAG + late * NU:
                            sp.wait_ge(s["ring_free"], base + place["turn", late, c, 0] + 1)
                            place_rows(c)
                if next_exp:
                    sp.wait_ge(s["pv"], q * NU + NU)
                    load_exp_kv(q + 1, CHUNKS - 1)
                    load_exp_q(q + 1, CHUNKS - 1)

            slot(OPENING, -1, False, (True, True))
            with sp.Fori(0, QUADS - 2) as q:
                slot(MIDDLE, q, True, (True, True))
            slot(MIDDLE, QUADS - 2, True, (True, False))
            slot(CLOSING, QUADS - 1, False, (False, False))

        @block.sync
        def _(sp):
            for c in range(CHUNKS):
                sp.dma_start(x_c[c], x_dram[:, TPC * c:TPC * (c + 1), :]).then_inc(load[f"x{c}"], 16)
            sp.dma_start(w_qkv_sb[:, :], wqkvT).then_inc(load["w_qkv"], 16)
            sp.dma_start(w_out_sb[:, 0, :], woT).then_inc(load["w_o"], 16)
            for dst, src in ((w_k_sb[:, :], wk), (bk_sb[:, :], bk), (bf_sb[:, :], bf.partition_broadcast(P))):
                sp.dma_start(dst, src).then_inc(load["w_b"], 16)
            sp.dma_start(w1_sb[:, :, :], w1.rearrange("e d h -> d e h")).then_inc(load["w_ffn"], 16)
            sp.dma_start(w2_sb[:, :, :], w2.rearrange("(m p) d -> p m d", p=P)).then_inc(load["w_ffn"], 16)
            sp.dma_start(b1_sb[:, :], b1).then_inc(load["w_ffn"], 16)
            sp.dma_start(gate_sb[:, :], gateT).then_inc(load["w_ffn"], 16)
            sp.dma_start(b2_sb[:, :, :], b2.partition_broadcast(P)).then_inc(load["w_ffn"], 16)
            sync_rows(sp, "a")
            sync_quads(sp, "a")
            sp.wait_ge(att["a"]["projected"], CHUNKS)
            sp.dma_start(w_v_sb, wv).then_inc(load["w_b"], 16)
            sp.dma_start(bv_sb, bv.partition_broadcast(P)).then_inc(load["w_b"], 16)
            sp.dma_start(w_out_sb[:, :, :], wf.rearrange("(g p) o -> p g o", p=P)).then_inc(load["w_f"], 16)
            sync_rows(sp, "b")
            sync_quads(sp, "b")
            for c in range(CHUNKS):
                sp.wait_ge(ffn[1]["out"], c + 1)
                sp.dma_start(out_dram[:, TPC * c:TPC * (c + 1), :], x_c[c]).then_inc(load["x0"], 16)
            sp.wait_ge(load["x0"], 16 * (1 + CHUNKS))

        LOAD_WEIGHTS_B = 5 * 16
        LOAD_WEIGHTS_FFN = 5 * 16
        TWO_BF16_ONES = float(np.array([0x3F803F80], np.uint32).view(np.float32)[0])

        def pool_pads(pool, kind):
            s = att[kind]
            for i, value in enumerate((0.0, 0.0, TWO_BF16_ONES, 0.0)):
                words = arena[:, i * half:(i + 1) * half]
                if i:
                    pool.wait_ge(s["pads"], 2 * i)
                pool.memset(words[32:64, :], value).then_inc(s["pads"], 1)
                pool.wait_ge(s["pads"], 2 * i + 1)
                pool.memset(words[64:128, :], value).then_inc(s["pads"], 1)
            pool.wait_ge(s["pads"], 8)

        def pool_low(pool, kind):
            s = att[kind]
            for c in range(CHUNKS):
                for w in range(2):
                    pool.wait_ge(s["mid"], 2 * c + w + 1)
                    pool.tensor_tensor(parts[:, c, w, 2, :], rest[:, c % 2, w, :], parts[:, c, w, 1, :],
                                       ALU.subtract).then_inc(s["low"], 1)

        def pool_quads(pool, kind):
            s = att[kind]

            def quad(q):
                for n, (c, kt) in enumerate(UNITS):
                    if kt >= TPC * c:
                        pool.wait_ge(s["exp"], q * 2 * NU + 2 * n + 2)
                        pool.wait_ge(s["kept"], q * diagonals(NU) + diagonals(n) + 1)
                        pool.tensor_tensor(carry[:, :], carry[:, :], carry[:, :], ALU.mult)
                        diagonal = probs[:, n % 2, :, 0:P]
                        pool.affine_select(out=diagonal, in_=diagonal, compare_op=ALU.is_ge, fill=0.0, base=0,
                                           pattern=[[0, QUAD], [1, P]], channel_multiplier=-1).then_inc(s["kept"], 1)

            pool.memset(carry[:, :], 0.0).then_inc(s["kept"], 1)
            with pool.Fori(0, QUADS) as q:
                quad(q)

        def pool_plus_bias(pool, i):
            s = ffn[i]
            for c in range(CHUNKS):
                pool.wait_ge(s["y"], TPC * (c + 1))
                pool.tensor_tensor(x_c[c], x_c[c], b2_sum[:, :, :].to_broadcast([P, TPC, D]),
                                   ALU.add).then_inc(s["x_bias"], 1)

        @block.gpsimd
        def _(pool):
            pool.memset(ones[:, :], 1.0).then_inc(const["ones"], 1)
            pool.memset(carry[:, :], 0.0)
            pool.memset(neg_max[:, :, :], 0.0).then_inc(const["zero"], 1)
            pool.memset(above[:, :], 0.0).then_inc(const["zero"], 1)
            pool.wait_ge(const["zero"], 2)
            pool.wait_ge(const["ones"], 1)
            pool.affine_select(out=ident[:, :], in_=ones[:, :], compare_op=ALU.is_equal, fill=0.0, base=0,
                               pattern=[[1, P]], channel_multiplier=-1).then_inc(const["ident"], 1)
            pool.affine_select(out=above[:, :], in_=above[:, :], compare_op=ALU.is_ge, fill=-3e38, base=0,
                               pattern=[[-1, P]], channel_multiplier=1).then_inc(const["above"], 1)
            pool.wait_ge(const["ident"], 1)
            pool.tensor_copy(ident_b[:, :], ident[:, :]).then_inc(const["ident"], 1)
            pool.tensor_copy(by_width[:, :].rearrange("p (d h) -> p d h", h=HEADS),
                             ident[:, :].rearrange("p (h d) -> p d h", h=HEADS)).then_inc(const["ident"], 1)
            pool.memset(v_all[:, :, :], 1.0).then_inc(const["v_ones"], 1)
            pool.wait_ge(const["v_ones"], 1)
            pool_pads(pool, "a")
            pool_low(pool, "a")
            pool.wait_ge(load["w_ffn"], LOAD_WEIGHTS_FFN)
            pool.tensor_tensor(b2_sum[:, 0, :], b2_sb[:, 0, :], b2_sb[:, 1, :], ALU.add).then_inc(const["b2"], 1)
            pool.wait_ge(const["b2"], 1)
            pool.tensor_tensor(b2_sum[:, 0, :], b2_sum[:, 0, :], b2_sb[:, 2, :], ALU.add).then_inc(const["b2"], 1)
            pool.tensor_tensor(gate_sb[:, 1:2], gate_sb[:, 1:2], gate_sb[:, 0:1], ALU.subtract).then_inc(const["gate"], 1)
            pool.wait_ge(const["gate"], 1)
            pool.tensor_scalar(gate_diff[:, :], ones[:, :], gate_sb[:, 1:2], None, ALU.mult).then_inc(const["gate"], 1)
            pool_quads(pool, "a")
            pool.wait_ge(const["b2"], 2)
            pool_plus_bias(pool, 0)
            pool_low(pool, "b")
            pool.wait_ge(ffn[0]["down"], CHUNKS)
            pool.wait_ge(att["b"]["v_stored"], TILES)
            pool.wait_ge(att["b"]["low"], 2 * CHUNKS)
            pool_pads(pool, "b")
            pool.wait_ge(load["w_b"], LOAD_WEIGHTS_B)
            for c in range(CHUNKS):
                pool.wait_ge(att["b"]["y"], TPC * (c + 1))
                pool.tensor_tensor(x_c[c], x_c[c], y_c[c], ALU.add).then_inc(att["b"]["x_plus"], 1)
                pool.wait_ge(att["b"]["x_plus"], 2 * c + 1)
                pool.tensor_tensor(x_c[c], x_c[c], bf_sb[:, :].rearrange("p (t d) -> p t d", t=1).to_broadcast([P, TPC, D]),
                                   ALU.add).then_inc(att["b"]["x_plus"], 1)
            pool_quads(pool, "b")
            pool_plus_bias(pool, 1)

        def pe_turn(pe, s, c, to):
            pe.wait_ge(s["y"], TPC * (c + 1))
            for t in range(TPC):
                last = nc.tensor.transpose(tiles_of(bank[to])[:, t, :], y[:, TPC * c + t, :], ident[:, :])
            last.then_inc(s["turned"], 1)

        def pe_project(pe, kind):
            s = att[kind]
            if kind == "a":
                pe.wait_ge(const["ident"], 1)
                pe.wait_ge(load["w_qkv"], 16)
            else:
                pe.wait_ge(load["w_b"], LOAD_WEIGHTS_B)
                pe.wait_ge(const["ident"], 3)
                pe.wait_ge(ffn[0]["out"], CHUNKS)
            for c in range(CHUNKS):
                if c >= 1:
                    pe.wait_ge(s["yT"], c)
                pe_turn(pe, s, c, 0)
                tokens = yT[:, c * CHUNK:(c + 1) * CHUNK]
                if c >= 1:
                    pe.wait_ge(s["rest"], 2 * c)
                pe.wait_ge(s["yT"], c + 1)
                if kind == "a":
                    nc.tensor.matmul(bank[2], w_qkv_sb[:, 0:D], tokens, start=True, stop=True).then_inc(s["qk"], 1)
                    nc.tensor.matmul(bank[3], w_qkv_sb[:, D:2 * D], tokens, start=True, stop=True).then_inc(s["qk"], 1)
                    if c >= 1:
                        pe.wait_ge(s["v_stored"], c)
                    for t in range(TPC):
                        last = nc.tensor.matmul(tiles_of(bank[4])[:, t, :], tokens[:, t * P:(t + 1) * P],
                                                w_qkv_sb[:, 2 * D:3 * D], start=True, stop=True)
                    last.then_inc(s["v"], 1)
                else:
                    nc.tensor.matmul(bank[2], by_width[:, :], tokens, start=True, stop=True).then_inc(s["qk"], 1)
                    nc.tensor.matmul(bank[3], w_k_sb[:, :], tokens, start=True, stop=True).then_inc(s["qk"], 1)
                    for t in range(TPC):
                        if c >= 1:
                            pe.wait_ge(s["v_stored"], TPC * (c - 1) + t + 1)
                        nc.tensor.matmul(bank[4 + t], tokens[:, t * P:(t + 1) * P], w_v_sb,
                                         start=True, stop=True).then_inc(s["v"], 1)

        def pe_quads(pe, kind):
            s = att[kind]

            size = 8 - RING[kind]

            def ring_turn(stretch, base, e):
                if not early(stretch, e, size):
                    pe.wait_ge(s["ring_free"], base + e + 1 - size)
                return ring_bank(kind, stretch, e)

            def maxima(stretch, k, base, e, n, h):
                c, kc, i = COMBO[n]
                if n == FIRST[c] and h == 0:
                    pe.wait_ge(s[f"m{c}"], k * 32 + 32)
                w = CHUNK if kc < c else (i + 1) * P
                to = ring_turn(stretch, base, e)
                last = nc.tensor.matmul(to[:, 0:w], q_max[:, c, h, i * P:(i + 1) * P],
                                        k_max[:, kc, h, 0:w], start=True, stop=kc < c)
                if kc == c:
                    last = nc.tensor.matmul(to[:, w - P:w], ident_b[:, :], above[:, :], start=False, stop=True)
                last.then_inc(s["ring_full"], 1)

            def turn(stretch, k, base, e, c):
                pe.wait_ge(s["neg_max"], k * CHUNKS + c + 1)
                to = ring_turn(stretch, base, e)
                nc.tensor.transpose(to.bitcast(BF16)[:, 0:P], neg_max[:, :, :].rearrange("p a b -> p (a b)"),
                                    ident_b[:, :]).then_inc(s["ring_full"], 1)

            def scores(q, n, pair):
                c, kt = UNITS[n]
                w, o = width(c, kt)
                if kt == 0 and pair == 0:
                    pe.wait_ge(s[f"s{c}"], q * 48 + 48)
                    pe.wait_ge(s[f"r{c}"], q * 16 + 16)
                if n >= 1:
                    pe.wait_ge(s["exp"], q * 2 * NU + 2 * (n - 1) + pair + 1)
                for h in (2 * pair, 2 * pair + 1):
                    last = nc.tensor.matmul(bank[SCORE + h][:, 0:w], k_exp[:, kt // TPC, h, kt % TPC * P:(kt % TPC + 1) * P],
                                            q_exp[:, c, h, o:CHUNK], start=True, stop=True)
                last.then_inc(s["scores"], 1)

            def values(q, n):
                c, kt = UNITS[n]
                w, o = width(c, kt)
                pe.wait_ge(s["exp"], q * 2 * NU + 2 * n + 2)
                if kt >= TPC * c:
                    pe.wait_ge(s["kept"], q * diagonals(NU) + diagonals(n) + 2)
                if kt == 0:
                    pe.wait_ge(s["sums"], q * CHUNKS + c + 1)
                ends = kt == TPC * (c + 1) - 1
                for h in range(QUAD):
                    last = nc.tensor.matmul(bank[PV][32 * h:32 * h + 32, o:CHUNK], v_quad[:, kt, VW * h:VW * (h + 1)],
                                            probs[:, n % 2, h, 0:w], start=kt == 0, stop=ends)
                if kind == "b":
                    for h in range(QUAD):
                        last = nc.tensor.matmul(bank[DEN][32 * h:32 * h + 32, o:CHUNK], ones[:, 0:VW],
                                                probs[:, n % 2, h, 0:w], start=kt == 0, stop=ends)
                last.then_inc(s["pv"], 1)

            def out_turn(stretch, q, base, e, c, which):
                pe.wait_ge(s["sums"], q * CHUNKS + c + 2)
                to = ring_turn(stretch, base, e)
                for t in range(TPC):
                    last = nc.tensor.transpose(tiles_of(to)[:, t, :], sums[:, which, t * P:(t + 1) * P],
                                               ident[:, :])
                last.then_inc(s["ring_full"], 1)

            def slot(stretch, q):
                place = ring(kind, stretch)
                base = ring_base(kind, stretch, q)
                for step in order(kind, stretch):
                    what, ahead, n, h = step
                    if what == "max":
                        maxima(stretch, q + ahead, base, place[step], n, h)
                    elif what == "turn":
                        turn(stretch, q + ahead, base, place[step], n)
                    elif what == "scores":
                        scores(q, n, h)
                    elif what == "values":
                        values(q, n)
                    else:
                        out_turn(stretch, q, base, place[step], n, int(what == "den"))

            if kind == "a":
                pe.wait_ge(const["ident"], 2)
                pe.wait_ge(const["ones"], 1)
                pe.wait_ge(const["above"], 1)
            pe.wait_ge(s["rest"], 2 * CHUNKS)
            pe.wait_ge(s["v_stored"], TILES if kind == "b" else CHUNKS)
            slot(OPENING, -1)
            with pe.Fori(0, QUADS - 1) as q:
                slot(MIDDLE, q)
            slot(CLOSING, QUADS - 1)

        def pe_out(pe, kind):
            s = att[kind]
            groups = 1 if kind == "a" else QUADS
            pe.wait_ge(load["w_o" if kind == "a" else "w_f"], 16)
            pe.wait_ge(s["o"], 1 + QUADS * CHUNKS)

            def turn_back(c):
                for g in range(groups):
                    if c >= 1:
                        pe.wait_ge(s["o_turned"], groups * (c - 1) + g + 1)
                    for t in range(TPC):
                        last = nc.tensor.transpose(tiles_of(bank[4 + g])[:, t, :],
                                                   o_tok[:, TPC * c + t, g * D:(g + 1) * D], ident[:, :])
                    last.then_inc(s["o_back"], 1)

            turn_back(0)
            for c in range(CHUNKS):
                if c < CHUNKS - 1:
                    turn_back(c + 1)
                pe.wait_ge(s["o_turned"], groups * (c + 1))
                for t in range(TPC):
                    for g in range(groups):
                        last = nc.tensor.matmul(tiles_of(bank[c])[:, t, :], turned_o[:, c % 2, g, t * P:(t + 1) * P],
                                                w_out_sb[:, g, :], start=g == 0, stop=g == groups - 1)
                last.then_inc(s["projected"], 1)

        def pe_ffn(pe, i):
            s = ffn[i]
            pe.wait_ge(load["w_ffn"], LOAD_WEIGHTS_FFN)
            pe.wait_ge(const["gate"], 2)
            before = att["ab"[i]]
            pe.wait_ge(before["x_done"], CHUNKS)

            def turn_and_gate(c):
                pe_turn(pe, s, c, 0)
                pe.wait_ge(s["yT"], c + 1)
                nc.tensor.matmul(bank[1], gate_diff[:, :], yT[:, c * CHUNK:(c + 1) * CHUNK],
                                 start=True, stop=True).then_inc(s["gate"], 1)

            turn_and_gate(0)
            for c in range(CHUNKS):
                for m in range(HCH):
                    e, j = divmod(m, HID // P)
                    u = c * HCH + m
                    if u >= 4:
                        pe.wait_ge(s["up_act" if u % 2 == 0 else "up_dve"], (u - 4) // 2 + 1)
                    if m == HID // P:
                        pe.wait_ge(s["masked"], 2 * (c + 1))
                    if e == 0:
                        tokens = yT[:, c * CHUNK:(c + 1) * CHUNK]
                    else:
                        tokens = masked[:, c % 2, e - 1, :]
                    nc.tensor.matmul(bank[4 + u % 4], w1_sb[:, e, j * P:(j + 1) * P], tokens,
                                     start=True, stop=True).then_inc(s["up"], 1)
                if c < CHUNKS - 1:
                    turn_and_gate(c + 1)
                pe.wait_ge(s["up_act"], HCH // 2 * (c + 1))
                pe.wait_ge(s["up_dve"], HCH // 2 * (c + 1))
                if c >= 2:
                    pe.wait_ge(s["out"], c - 1)
                for t in range(TPC):
                    for m in range(HCH):
                        last = nc.tensor.matmul(tiles_of(bank[2 + c % 2])[:, t, :], hidden[:, c % 2, m, t * P:(t + 1) * P],
                                                w2_sb[:, m, :], start=m == 0, stop=m == HCH - 1)
                last.then_inc(s["down"], 1)

        @block.tensor
        def _(pe):
            pe_project(pe, "a")
            pe_quads(pe, "a")
            pe_out(pe, "a")
            pe_ffn(pe, 0)
            pe_project(pe, "b")
            pe_quads(pe, "b")
            pe_out(pe, "b")
            pe_ffn(pe, 1)

        def act_sqrt(act, s):
            act.wait_ge(s["norm"], 2 * TILES + 1)
            nc.scalar.activation(deviation[:, :], rstd[:, :], ACT.Sqrt).then_inc(s["sqrt"], 1)

        def act_store_yT(act, s, c):
            act.wait_ge(s["turned"], c + 1)
            nc.scalar.copy(yT[:, c * CHUNK:(c + 1) * CHUNK], bank[0]).then_inc(s["yT"], 1)

        def act_project(act, kind):
            s = att[kind]
            act_sqrt(act, s)
            v_heads = v_all[:, :, :].rearrange("p t (h w) -> p t h w", h=HEADS)

            def high(c, w):
                act.wait_ge(s["qk"], 2 * c + w + 1)
                source = bank[2 + w]
                if kind == "b" and w == 1:
                    nc.scalar.activation(parts[:, c, w, 0, :], source, ACT.Identity, bias=bk_sb[:, 0:1]).then_inc(s["high"], 1)
                else:
                    nc.scalar.copy(parts[:, c, w, 0, :], source).then_inc(s["high"], 1)

            for c in range(CHUNKS):
                act_store_yT(act, s, c)
                high(c, 0)
                high(c, 1)
                if kind == "a":
                    if c == 0:
                        act.wait_ge(const["v_ones"], 1)
                    act.wait_ge(s["v"], c + 1)
                    nc.scalar.copy(v_heads[:, TPC * c:TPC * (c + 1), :, 0:HD],
                                   bank[4].rearrange("p (t h d) -> p t h d", t=TPC, h=HEADS)).then_inc(s["v_stored"], 1)
                for w in range(2):
                    act.wait_ge(s["rest"], 2 * c + w + 1)
                    nc.scalar.copy(parts[:, c, w, 1, :], rest[:, c % 2, w, :]).then_inc(s["mid"], 1)

        def act_quads(act, kind):
            s = att[kind]
            scale = HD ** -0.5 if kind == "a" else 1.0

            def copy_sums(q, c):
                act.wait_ge(s["pv"], q * NU + FIRST[c + 1])
                act.wait_ge(s["o"], q * CHUNKS + c + 1)
                banks = 1 if kind == "a" else 2
                nc.scalar.copy(sums[:, 0:banks, :], psum[:, PV:PV + banks, :]).then_inc(s["sums"], 1)

            def quad(q):
                for n, (c, kt) in enumerate(UNITS):
                    w, o = width(c, kt)
                    for pair in range(2):
                        act.wait_ge(s["scores"], q * 2 * NU + 2 * n + pair + 1)
                        if n >= 2 and pair == 0:
                            act.wait_ge(s["pv"], q * NU + n - 1)
                        heads = slice(2 * pair, 2 * pair + 2)
                        nc.scalar.activation(probs[:, n % 2, heads, 0:w], psum[:, SCORE + 2 * pair:SCORE + 2 * pair + 2, 0:w],
                                             ACT.Exp, scale=scale).then_inc(s["exp"], 1)
                    if n in FIRST[1:]:
                        copy_sums(q, FIRST.index(n) - 1)
                copy_sums(q, CHUNKS - 1)

            nc.scalar.copy(act_word[:, :], ones[0:1, 0:1]).then_inc(s["sums"], 1)
            act.wait_ge(s["low"], 2 * CHUNKS)
            for c in range(CHUNKS):
                act.wait_ge(s[f"rows{c}"], 2 * PARTS * 16)
            with act.Fori(0, QUADS) as q:
                quad(q)

        def act_out(act, kind):
            s = att[kind]
            groups = 1 if kind == "a" else QUADS
            for c in range(CHUNKS):
                for g in range(groups):
                    act.wait_ge(s["o_back"], groups * c + g + 1)
                    if c >= 2 and g == 0:
                        act.wait_ge(s["projected"], c - 1)
                    nc.scalar.activation(turned_o[:, c % 2, g, :], bank[4 + g],
                                         ACT.Gelu if kind == "b" else ACT.Copy).then_inc(s["o_turned"], 1)

        def act_ffn(act, i):
            s = ffn[i]
            act_sqrt(act, s)
            act_store_yT(act, s, 0)
            for c in range(CHUNKS):
                if c >= 2:
                    act.wait_ge(s["down"], c - 1)
                for m in range(0, HCH, 2):
                    u = c * HCH + m
                    act.wait_ge(s["up"], u + 1)
                    nc.scalar.activation(hidden[:, c % 2, m, :], bank[4 + u % 4], ACT.Relu,
                                         bias=b1_sb[:, m:m + 1]).then_inc(s["up_act"], 1)
                if c < CHUNKS - 1:
                    act_store_yT(act, s, c + 1)

        @block.scalar
        def _(act):
            act_project(act, "a")
            act_quads(act, "a")
            act_out(act, "a")
            act_ffn(act, 0)
            act_project(act, "b")
            act_quads(act, "b")
            act_out(act, "b")
            act_ffn(act, 1)

        def dve_norm(dve, s, ready):
            for t in range(TILES):
                if t % TPC == 0:
                    ready(t // TPC)
                nc.vector.bn_stats(stats[:, t, :], x[:, t, :]).then_inc(s["norm"], 1)
            for t in range(TILES):
                dve.wait_ge(s["norm"], t + 1)
                nc.vector.bn_aggr(mean_var[:, t, :], stats[:, t, :]).then_inc(s["norm"], 1)
            dve.wait_ge(s["norm"], 2 * TILES)
            nc.vector.tensor_scalar(rstd[:, :], mean_var[:, :, 1], EPS, None, ALU.add).then_inc(s["norm"], 1)
            dve.wait_ge(s["sqrt"], 1)
            nc.vector.reciprocal(rstd[:, :], deviation[:, :]).then_inc(s["norm"], 1)
            dve.wait_ge(s["norm"], 2 * TILES + 2)
            for t in range(TILES):
                nc.vector.tensor_scalar(y[:, t, :], x[:, t, :], mean_var[:, t, 0:1], rstd[:, t:t + 1],
                                        ALU.subtract, ALU.mult).then_inc(s["y"], 1)

        def dve_project(dve, kind):
            s = att[kind]
            for c in range(CHUNKS):
                for w in range(2):
                    dve.wait_ge(s["high"], 2 * c + w + 1)
                    if c >= 2:
                        dve.wait_ge(s["low"], 2 * (c - 2) + w + 1)
                    if kind == "b" and w == 1:
                        nc.vector.scalar_tensor_tensor(rest[:, c % 2, w, :], bank[3], bk_sb[:, 0:1], parts[:, c, w, 0, :],
                                                       ALU.add, ALU.subtract).then_inc(s["rest"], 1)
                    else:
                        nc.vector.tensor_tensor(rest[:, c % 2, w, :], bank[2 + w], parts[:, c, w, 0, :],
                                                ALU.subtract).then_inc(s["rest"], 1)
                if kind == "b":
                    for t in range(TPC):
                        dve.wait_ge(s["v"], TPC * c + t + 1)
                        nc.vector.tensor_tensor(v_all[:, TPC * c + t, :], bank[4 + t], bv_sb, ALU.add
                                                ).then_inc(s["v_stored"], 1)

        def dve_quads(dve, kind):
            s = att[kind]

            def maxima(stretch, k, base, e, n, h):
                c, kc, i = COMBO[n]
                if n == FIRST[c] and h == 0:
                    if not (isinstance(k, int) and k == 0 and c == 0):
                        dve.wait_ge(s["folded"], k * CHUNKS + c)
                    nc.vector.memset(max_parts[:, :, :, :], -3e38).then_inc(s["cleared"], 1)
                    dve.wait_ge(s["cleared"], k * CHUNKS + c + 1)
                w = CHUNK if kc < c else (i + 1) * P
                dve.wait_ge(s["ring_full"], base + e + 1)
                nc.vector.tensor_reduce(max_parts[:, h, i, kc:kc + 1], ring_bank(kind, stretch, e)[:, 0:w],
                                        AX.X, ALU.max).then_inc(s["ring_free"], 1)
                if n + 1 in FIRST and h == QUAD - 1:
                    fold(k, c, base + e + 1)

            def fold(k, c, entries):
                dve.wait_ge(s["ring_free"], entries)
                nc.vector.tensor_reduce(row_max[:, :].rearrange("p (h i) -> p h i", h=QUAD), max_parts[:, :, :, :],
                                        AX.X, ALU.max).then_inc(s["folded"], 1)
                dve.wait_ge(s["folded"], k * CHUNKS + c + 1)
                nc.vector.tensor_scalar(neg_max[:, 0, :], row_max[:, :], -1.0, None, ALU.mult).then_inc(s["split"], 1)
                dve.wait_ge(s["split"], (k * CHUNKS + c) * 3 + 1)
                nc.vector.scalar_tensor_tensor(max_rest[:, :], row_max[:, :], -1.0, neg_max[:, 0, :],
                                               ALU.mult, ALU.subtract).then_inc(s["split"], 1)
                dve.wait_ge(s["split"], (k * CHUNKS + c) * 3 + 2)
                nc.vector.tensor_copy(neg_max[:, 1, :], max_rest[:, :]).then_inc(s["split"], 1)
                dve.wait_ge(s["split"], (k * CHUNKS + c) * 3 + 3)
                nc.vector.tensor_tensor(neg_max[:, 2, :], max_rest[:, :], neg_max[:, 1, :], ALU.subtract).then_inc(s["neg_max"], 1)

            def turn(stretch, k, base, e, c):
                dve.wait_ge(s["ring_full"], base + e + 1)
                if not (isinstance(k, int) and k == 0):
                    dve.wait_ge(s[f"r{c}"], k * 16)
                nc.vector.tensor_copy(max_rows[:, c, :], ring_bank(kind, stretch, e).bitcast(BF16)[0:PARTS * QUAD * TPC, 0:P]
                                      ).then_inc(s["ring_free"], 1)

            def denominators(stretch, q, base, e, c):
                dve.wait_ge(s["ring_full"], base + e + 1)
                dve.wait_ge(s["o"], q * CHUNKS + c + 1)
                column = HD if kind == "a" else 0
                inverse = nc.vector.reciprocal(recip[:, :, :, :], ring_bank(kind, stretch, e).rearrange(
                    "p (t h d) -> p t h d", t=TPC, h=QUAD)[:, :, :, column:column + 1])
                if kind == "a":
                    inverse.then_inc(s["recip"], 1)
                else:
                    inverse.then_inc(s["ring_free"], 1)

            def normalise(stretch, q, base, e, c):
                wide = HD if kind == "a" else VW
                if kind == "a":
                    denominators(stretch, q, base, e, c)
                    dve.wait_ge(s["recip"], q * CHUNKS + c + 1)
                else:
                    dve.wait_ge(s["ring_full"], base + e + 1)
                    dve.wait_ge(s["ring_free"], base + e)
                values = ring_bank(kind, stretch, e).rearrange("p (t h d) -> p t h d", t=TPC, h=QUAD)[:, :, :, 0:wide]
                o = o_tok[:, TPC * c:TPC * (c + 1), bass.ds(q * QUAD * wide, QUAD * wide)]
                nc.vector.tensor_tensor(o.rearrange("p t (h d) -> p t h d", h=QUAD), values,
                                        recip[:, :, :, :].to_broadcast([P, TPC, QUAD, wide]), ALU.mult).then_inc(s["o"], 1)
                dve.wait_ge(s["o"], q * CHUNKS + c + 2)
                nc.vector.memset(dve_word[:, :], 0.0).then_inc(s["ring_free"], 1)

            def slot(stretch, q):
                base = ring_base(kind, stretch, q)
                for step, e in ring(kind, stretch).items():
                    what, ahead, n, h = step
                    if what == "max":
                        maxima(stretch, q + ahead, base, e, n, h)
                    elif what == "turn":
                        turn(stretch, q + ahead, base, e, n)
                    elif what == "den":
                        denominators(stretch, q, base, e, n)
                    else:
                        normalise(stretch, q, base, e, n)

            if kind == "a":
                dve.wait_ge(const["b2"], 2)
            nc.vector.memset(dve_word[:, :], 0.0).then_inc(s["o"], 1)
            slot(OPENING, -1)
            with dve.Fori(0, QUADS - 1) as q:
                slot(MIDDLE, q)
            slot(CLOSING, QUADS - 1)

        def dve_add(dve, s, c, done, count, source):
            dve.wait_ge(s[done], count)
            return nc.vector.tensor_tensor(x_c[c], tiles_of(source), x_c[c], ALU.add)

        def dve_ffn(dve, i):
            s = ffn[i]
            before = att["ab"[i]]
            dve_norm(dve, s, lambda c: dve.wait_ge(before["x_done"], c + 1))

            def mask(c):
                dve.wait_ge(s["gate"], c + 1)
                tokens = yT[:, c * CHUNK:(c + 1) * CHUNK]
                for e, chooses in enumerate((ALU.is_le, ALU.is_gt)):
                    nc.vector.scalar_tensor_tensor(masked[:, c % 2, e, :], bank[1], 0.0, tokens,
                                                   chooses, ALU.mult).then_inc(s["masked"], 1)

            mask(0)
            for c in range(CHUNKS):
                if c >= 2:
                    dve.wait_ge(s["down"], c - 1)
                for m in range(1, HCH, 2):
                    u = c * HCH + m
                    dve.wait_ge(s["up"], u + 1)
                    nc.vector.tensor_scalar(hidden[:, c % 2, m, :], bank[4 + u % 4], b1_sb[:, m:m + 1], 0.0,
                                            ALU.add, ALU.max).then_inc(s["up_dve"], 1)
                if c < CHUNKS - 1:
                    mask(c + 1)
                dve.wait_ge(s["x_bias"], c + 1)
                dve_add(dve, s, c, "down", c + 1, bank[2 + c % 2]).then_inc(s["out"], 1)

        @block.vector
        def _(dve):
            dve_norm(dve, att["a"], lambda c: dve.wait_ge(load[f"x{c}"], 16))
            dve_project(dve, "a")
            dve_quads(dve, "a")
            for c in range(CHUNKS):
                dve_add(dve, att["a"], c, "projected", c + 1, bank[c]).then_inc(att["a"]["x_done"], 1)
            dve_ffn(dve, 0)
            dve_norm(dve, att["b"], lambda c: dve.wait_ge(ffn[0]["out"], c + 1))
            dve_project(dve, "b")
            dve_quads(dve, "b")
            dve.wait_ge(att["b"]["x_plus"], 2 * CHUNKS)
            for c in range(CHUNKS):
                dve_add(dve, att["b"], c, "projected", c + 1, bank[c]).then_inc(att["b"]["x_done"], 1)
            dve_ffn(dve, 1)


def kernel(**inputs):
    from concourse import bacc
    from concourse.bass_utils import run_bass_kernel_spmd

    a = {k: np.ascontiguousarray(v) for k, v in inputs.items()}

    def by_width(w):
        return w.reshape(w.shape[0], HEADS, HD).transpose(0, 2, 1).reshape(w.shape)

    w_qkv = a["L0_attn_a_w_qkv"].T
    arrays = {
        "x_in": a["L0_attn_a_x"].reshape(S, D),
        "wqkvT": np.concatenate([by_width(w_qkv[:, :D]), by_width(w_qkv[:, D:2 * D]), w_qkv[:, 2 * D:]], 1),
        "woT": a["L0_attn_a_w_out"].T,
        "wk": by_width(a["L0_attn_b_Wk"]),
        "bk": by_width(a["L0_attn_b_bk"].reshape(1, D)).T,
        "wv": a["L0_attn_b_Wv"],
        "bv": a["L0_attn_b_bv"],
        "wf": a["L0_attn_b_Wf"],
        "bf": a["L0_attn_b_bf"],
        "gateT": a["L0_ffn_gate_w"].T,
        "w1": np.concatenate([a["L0_ffn_sw1"][None], a["L0_ffn_w1"]]),
        "b1": np.concatenate([a["L0_ffn_sb1"][None], a["L0_ffn_b1"]]).reshape(HCH, P).T,
        "w2": np.concatenate([a["L0_ffn_sw2"], a["L0_ffn_w2"].reshape(-1, D)]),
        "b2": np.concatenate([a["L0_ffn_sb2"][None], a["L0_ffn_b2"]]),
    }
    nc = bacc.Bacc("TRN2", target_bir_lowering=False, num_devices=1)
    maps, args = {}, []
    for name, array in arrays.items():
        array = np.ascontiguousarray(array)
        maps[f"in_{name}"] = array
        args.append(nc.dram_tensor(f"in_{name}", array.shape, mybir.dt.from_np(array.dtype), kind="ExternalInput").ap())
    out = nc.dram_tensor("out_x", (S, D), F32, kind="ExternalOutput").ap()
    build(nc, *args, out)
    result = run_bass_kernel_spmd(nc, [maps], core_ids=[0])
    return result.results[0]["out_x"].reshape(1, S, D)
```

```python
from contextlib import ExitStack

import concourse.bass as bass
import numpy as np
from concourse import mybir

F32 = mybir.dt.float32
BF16 = mybir.dt.bfloat16
ALU = mybir.AluOpType
ACT = mybir.ActivationFunctionType
AX = mybir.AxisListType

P = 128
S = 2048
D = 128
HEADS = 16
HD = D // HEADS
QUAD = 4
QUADS = HEADS // QUAD
TILES = S // P
CHUNK = 512
CHUNKS = S // CHUNK
TPC = CHUNK // P
VW = 32
HID = 512
EXPERTS = 3
HCH = EXPERTS * HID // P
EPS = 1e-5

PAIRS = [(0, 2), (0, 1), (0, 0), (1, 0), (2, 0), (1, 1)]
COMBOS = len(PAIRS)
ROWS = COMBOS * HD
PARTS = 3

UNITS = [(c, kt) for c in range(CHUNKS) for kt in range(TPC * (c + 1))]
NU = len(UNITS)
FIRST = [UNITS.index((c, 0)) for c in range(CHUNKS)] + [NU]
COMBO = [(c, kc, i) for c in range(CHUNKS) for kc in range(c + 1) for i in range(TPC)]
LEAD = 20
SPLIT_LAG, TURN_LAG, OUT_LAG = 0, 2, 2
SLOT = [n % 3 for n in range(NU - 1)] + [1]
SUMMED = [n for n, (c, kt) in enumerate(UNITS) if kt < TPC * c and (kt == 0 or kt % 2 == 1) and kt < TPC * c - 1]
OPENING, MIDDLE, CLOSING = range(3)


def order(kind, stretch):
    exps = stretch != OPENING
    out = ("out",) if kind == "a" else ("den", "out")
    steps = []
    for n in range(LEAD if stretch == OPENING else 0, NU):
        ahead, m = divmod(n + LEAD, NU)
        for late in (0, 1):
            for c in range(CHUNKS):
                if n + LEAD == FIRST[c + 1] + TURN_LAG + late * NU and (stretch == MIDDLE or late == (stretch == OPENING)):
                    steps.append(("turn", late, c, 0))
        with_max = stretch == MIDDLE or ahead == (stretch == OPENING)
        tiles = [("max", ahead, m, h) if with_max else None for h in range(QUAD)]
        scores = [("scores", 0, n, pair) for pair in range(2)] if exps else [None, None]
        if kind == "a":
            steps += [scores[0], tiles[0], scores[1], tiles[1], tiles[2]]
        else:
            steps += [tiles[0], scores[0], tiles[1], scores[1], tiles[2]]
        tile_first = kind == "b" and n - 1 in SUMMED
        if tile_first:
            steps.append(tiles[3])
        if exps and n >= 1:
            steps.append(("values", 0, n - 1, 0))
        if exps and n == NU - 1:
            steps += [("ones", 0, n - 1, 0), ("values", 0, n, 0), ("ones", 0, n, 0)]
        if exps and n - OUT_LAG in FIRST[1:] and kind == "b":
            steps.append(("den", 0, FIRST.index(n - OUT_LAG) - 1, 0))
        if not tile_first:
            steps.append(tiles[3])
        if exps and 1 <= n < NU - 1:
            steps.append(("ones", 0, n - 1, 0))
        if exps and n - OUT_LAG in FIRST[1:]:
            steps.append(("out", 0, FIRST.index(n - OUT_LAG) - 1, 0))
    if exps:
        steps += [(what, 0, CHUNKS - 1, 0) for what in out]
    return [x for x in steps if x]


def ring(kind, stretch):
    turns = [x for x in order(kind, stretch) if x[0] in ("max", "turn", "den", "out")]
    return {x: e for e, x in enumerate(turns)}


def ring_base(kind, stretch, q):
    if stretch == OPENING:
        return 0
    return len(ring(kind, OPENING)) + q * len(ring(kind, MIDDLE))


def width(c, kt):
    o = max(0, kt - TPC * c) * P
    return CHUNK - o, o


def diagonals(n):
    return sum(1 for c, kt in UNITS[:n] if kt >= TPC * c)


def adds(n):
    return sum(1 for m in SUMMED if m < n and UNITS[m][1] > 0)


def build(nc, x_in, wqkvT, woT, wk, bk, wv, bv, wf, bf, gateT, w1, b1, w2, b2, out):
    ctx = ExitStack()
    with ctx:
        def sb(name, shape, dt=F32):
            return ctx.enter_context(nc.sbuf_tensor(name, shape, dt))

        def sems(stage, names):
            return {n: ctx.enter_context(nc.semaphore(f"{stage}_{n}")) for n in names.split()}

        x = sb("x", [P, TILES, D])
        y = sb("y", [P, TILES, D])
        yT = sb("yT", [P, S])
        arena = sb("arena", [P, 4 * S * 2])
        probs_mem = sb("probs_mem", [P, 6144])
        v_quad = sb("v_quad", [P, TILES, QUAD * VW])
        vo_mem = sb("vo_mem", [P, 2 * TILES, HEADS * VW])
        w_qkv_sb = sb("w_qkv_sb", [P, 3 * D])
        w_out_sb = sb("w_out_sb", [P, QUADS, D])
        w_k_sb = sb("w_k_sb", [P, D])
        w1_sb = sb("w1_sb", [P, EXPERTS, HID])
        w2_sb = sb("w2_sb", [P, HCH, D])
        b1_sb = sb("b1_sb", [P, HCH])
        bk_sb = sb("bk_sb", [P, 1])
        bf_sb = sb("bf_sb", [P, D])
        b2_sum = sb("b2_sum", [P, 1, D])
        gate_sb = sb("gate_sb", [P, 2])
        gate_diff = sb("gate_diff", [P, D])
        ones = sb("ones", [P, P])
        ident = sb("ident", [P, P])
        by_width = sb("by_width", [P, P])
        ident_b = sb("ident_b", [P, P], BF16)
        above = sb("above", [P, P], BF16)
        stats = sb("stats", [P, TILES, 6])
        mean_var = sb("mean_var", [P, TILES, 2])
        deviation = sb("deviation", [P, TILES])
        rstd = sb("rstd", [P, TILES])
        max_parts = sb("max_parts", [P, QUAD, TPC, CHUNKS])
        row_max = sb("row_max", [P, QUAD * TPC])
        max_rest = sb("max_rest", [P, QUAD * TPC])
        max_split = sb("max_split", [P, P // (QUAD * TPC), QUAD * TPC], BF16)
        zeros = sb("zeros", [P, QUAD * TPC])
        max_rows = sb("max_rows", [PARTS * QUAD * TPC, CHUNKS, P], BF16)
        carry, act_word, dve_word = (sb(n, [1, 1]) for n in ("carry", "act_word", "dve_word"))

        half = S * 2
        operands = [arena[:, i * half:(i + 1) * half].bitcast(BF16).rearrange("p (c h t) -> p c h t", c=CHUNKS, h=QUAD)
                    for i in range(4)]
        q_exp, q_max, k_exp, k_max = operands
        v_all = vo_mem[:, 0:TILES, :]
        o_tok = vo_mem[:, TILES:2 * TILES, :]
        hidden = [vo_mem[:, b * TILES:b * TILES + HCH, :] for b in range(2)]
        w_v_sb = o_tok[:, HCH, :]
        bv_sb = o_tok[:, HCH + 1, :]
        b2_sb = o_tok[:, 0, 0:3 * D].rearrange("p (e d) -> p e d", e=3)
        probs = probs_mem[:, :].rearrange("p (b h t) -> p b h t", b=3, h=QUAD)
        prob_sum = y[:, :, :].rearrange("p t d -> p (t d)").rearrange("p (h t) -> p h t", h=QUAD)
        parts = probs_mem[:, :].bitcast(BF16).rearrange("p (c w r t) -> p c w r t", c=CHUNKS, w=2, r=PARTS)
        rest = v_quad[:, :, :].rearrange("p t n -> p (t n)").rearrange("p (b w t) -> p b w t", b=2, w=2)
        masked = probs_mem[:, 0:2048].rearrange("p (b e t) -> p b e t", b=2, e=2)
        sums = yT[:, 0:2 * CHUNK].rearrange("p (w t) -> p w t", w=2)
        recip = sb("recip", [P, TPC, QUAD, 1])
        o_heads = o_tok[:, :, :].rearrange("p t (h d) -> p t h d", h=HEADS)
        o_narrow = o_tok[:, :, 0:D]
        turned_o = probs_mem[:, 0:4096].rearrange("p (b g t) -> p b g t", b=2, g=QUADS)
        x_c = [x[:, TPC * c:TPC * (c + 1), :] for c in range(CHUNKS)]
        y_c = [y[:, TPC * c:TPC * (c + 1), :] for c in range(CHUNKS)]

        psum = ctx.enter_context(nc.psum_tensor("psum", [P, 8, CHUNK], F32))
        bank = [psum[:, i, :] for i in range(8)]
        tiles_of = lambda b: b.rearrange("p (t d) -> p t d", t=TPC)
        SCORE, PV, DEN = 0, 4, 5
        RING = {"a": 5, "b": 6}

        def ring_bank(kind, stretch, e):
            size = 8 - RING[kind]
            assert len(ring(kind, MIDDLE)) % size == 0
            return bank[RING[kind] + (ring_base(kind, stretch, 0) + e) % size]

        def early(stretch, e, turns):
            return stretch == OPENING and e < turns

        scratch = {s: [nc.dram_tensor(f"rows_{s}_{w}", (ROWS, HEADS, S), BF16).ap() for w in "qk"]
                   for s in "ab"}
        x_dram = x_in.rearrange("(t p) d -> p t d", p=P)
        out_dram = out.rearrange("(t p) d -> p t d", p=P)

        load = sems("load", "x0 x1 x2 x3 w_qkv w_o w_f w_b w_ffn")
        const = sems("const", "zero ones ident above gate bias b2 v_ones pads")
        norm_names = "norm sqrt rstd y turned yT "
        ffn = [sems(f"ffn{i}", norm_names + "gate masked up up_act up_dve down down_read x_bias out")
               for i in range(2)]
        att = {s: sems(f"att_{s}", norm_names +
                       "qk high rest mid low v v_stored rows0 rows1 rows2 rows3 x_plus "
                       "m0 m1 m2 m3 s0 s1 s2 s3 r0 r1 r2 r3 "
                       "scores exp kept summed pv ring_full ring_free folded split "
                       "max_split sums recip o o_back o_turned projected x_done") for s in "ab"}

        block = ctx.enter_context(nc.Block())

        def sync_rows(sp, kind, c):
            s = att[kind]
            tokens = slice(c * CHUNK, (c + 1) * CHUNK)
            sp.wait_ge(s["low"], 2 * (c + 1))
            sp.wait_ge(s["mid"], 2 * (c + 1))
            for w in range(2):
                for part in range(PARTS):
                    blocks = [b for b, pair in enumerate(PAIRS) if pair[w] == part]
                    step = blocks[1] - blocks[0] if len(blocks) > 1 else 1
                    rows = scratch[kind][w].rearrange("(b d) h t -> (d h) b t", b=COMBOS)[
                        :, blocks[0]:blocks[-1] + 1:step, tokens]
                    source = parts[:, c, w, part:part + 1, :].to_broadcast([P, len(blocks), CHUNK])
                    sp.dma_start(rows, source).then_inc(s[f"rows{c}"], 16)

        def sync_quads(sp, kind):
            s = att[kind]
            rows_q, rows_k = scratch[kind]

            def piece(rows, quad, c):
                return rows[:, bass.ds(quad * QUAD, QUAD), c * CHUNK:(c + 1) * CHUNK]

            def load_max_q(quad, c):
                sp.dma_start(q_max[0:ROWS, c, :, :], piece(rows_q, quad, c)).then_inc(s[f"m{c}"], 16)

            def load_max_k(quad, c):
                sp.dma_start(k_max[0:ROWS, c, :, :], piece(rows_k, quad, c)).then_inc(s[f"m{c}"], 16)

            def load_exp_q(quad, c):
                sp.dma_start(q_exp[0:ROWS, c, :, :], piece(rows_q, quad, c)).then_inc(s[f"s{c}"], 16)

            def load_exp_kv(quad, c):
                sp.dma_start(v_quad[:, TPC * c:TPC * (c + 1), :],
                             v_all[:, TPC * c:TPC * (c + 1), bass.ds(quad * QUAD * VW, QUAD * VW)]).then_inc(s[f"s{c}"], 16)
                sp.dma_start(k_exp[0:ROWS, c, :, :], piece(rows_k, quad, c)).then_inc(s[f"s{c}"], 16)

            def place_rows(c):
                sp.dma_start(q_exp[ROWS:ROWS + PARTS, c, :, :].rearrange("p h (i t) -> p (h i) t", i=TPC),
                             max_rows[:, c, :]).then_inc(s[f"r{c}"], 16)

            def first_max(c):
                sp.wait_ge(s[f"rows{c}"], 2 * PARTS * 16)
                load_max_q(0, c)
                load_max_k(0, c)

            sync_rows(sp, kind, 0)
            sync_rows(sp, kind, 1)
            sp.wait_ge(const["pads"], 4)
            first_max(0)
            for c in range(2, CHUNKS):
                sync_rows(sp, kind, c)
                first_max(c - 1)
            first_max(CHUNKS - 1)
            sp.wait_ge(s["v_stored"], TILES if kind == "b" else CHUNKS)
            sp.wait_ge(const["pads"], 8)
            for c in range(CHUNKS):
                load_exp_q(0, c)
                load_exp_kv(0, c)

            def slot(stretch, q, next_exp, next_max):
                place = ring(kind, stretch)
                base = ring_base(kind, stretch, q)
                for n in range(LEAD if stretch == OPENING else 0, NU):
                    ahead, m = divmod(n + LEAD, NU)
                    c, kc, i = COMBO[m]
                    if ("max", ahead, m, 0) in place and next_max[ahead] and i == TPC - 1:
                        if kc == c or (c == CHUNKS - 1 and kc > 0):
                            sp.wait_ge(s["ring_full"], base + place["max", ahead, m, QUAD - 1] + 1)
                        if c == CHUNKS - 1 and kc > 0:
                            load_max_k(q + ahead + 1, kc)
                        if c == CHUNKS - 1 and kc == 1:
                            load_max_k(q + ahead + 1, 0)
                        if kc == c:
                            load_max_q(q + ahead + 1, c)
                    if next_exp and n >= 1:
                        c, kt = UNITS[n - 1]
                        if c == CHUNKS - 1 and kt % TPC == TPC - 1:
                            sp.wait_ge(s["pv"], q * NU + n)
                            load_exp_kv(q + 1, kt // TPC)
                            load_exp_q(q + 1, kt // TPC)
                    for what, late, c, _ in place:
                        if what == "turn" and n + LEAD == FIRST[c + 1] + TURN_LAG + late * NU:
                            sp.wait_ge(s["ring_free"], base + place["turn", late, c, 0] + 1)
                            place_rows(c)
                if next_exp:
                    sp.wait_ge(s["pv"], q * NU + NU)
                    load_exp_kv(q + 1, CHUNKS - 1)
                    load_exp_q(q + 1, CHUNKS - 1)

            slot(OPENING, -1, False, (True, True))
            with sp.Fori(0, QUADS - 2) as q:
                slot(MIDDLE, q, True, (True, True))
            slot(MIDDLE, QUADS - 2, True, (True, False))
            slot(CLOSING, QUADS - 1, False, (False, False))

        @block.sync
        def _(sp):
            for c in range(CHUNKS):
                sp.dma_start(x_c[c], x_dram[:, TPC * c:TPC * (c + 1), :]).then_inc(load[f"x{c}"], 16)
            sp.dma_start(w_qkv_sb[:, :], wqkvT).then_inc(load["w_qkv"], 16)
            sp.dma_start(w_out_sb[:, 0, :], woT).then_inc(load["w_o"], 16)
            for dst, src in ((w_k_sb[:, :], wk), (bk_sb[:, :], bk), (bf_sb[:, :], bf.partition_broadcast(P))):
                sp.dma_start(dst, src).then_inc(load["w_b"], 16)
            sp.dma_start(w1_sb[:, :, :], w1.rearrange("e d h -> d e h")).then_inc(load["w_ffn"], 16)
            sp.dma_start(w2_sb[:, :, :], w2.rearrange("(m p) d -> p m d", p=P)).then_inc(load["w_ffn"], 16)
            sp.dma_start(b1_sb[:, :], b1).then_inc(load["w_ffn"], 16)
            sp.dma_start(gate_sb[:, :], gateT).then_inc(load["w_ffn"], 16)
            sp.dma_start(b2_sb[:, :, :], b2.partition_broadcast(P)).then_inc(load["w_ffn"], 16)
            sync_quads(sp, "a")
            sp.wait_ge(att["a"]["projected"], CHUNKS)
            sp.dma_start(w_v_sb, wv).then_inc(load["w_b"], 16)
            sp.dma_start(bv_sb, bv.partition_broadcast(P)).then_inc(load["w_b"], 16)
            sp.dma_start(w_out_sb[:, :, :], wf.rearrange("(g p) o -> p g o", p=P)).then_inc(load["w_f"], 16)
            sync_quads(sp, "b")
            for c in range(CHUNKS):
                sp.wait_ge(ffn[1]["out"], c + 1)
                sp.dma_start(out_dram[:, TPC * c:TPC * (c + 1), :], x_c[c]).then_inc(load["x0"], 16)
            sp.wait_ge(load["x0"], 16 * (1 + CHUNKS))

        NORM_STEPS = 2 * TPC + 1
        LOAD_WEIGHTS_B = 5 * 16
        LOAD_WEIGHTS_FFN = 5 * 16
        TWO_BF16_ONES = float(np.array([0x3F803F80], np.uint32).view(np.float32)[0])

        def pool_pads(pool):
            pads = ((q_max, 0.0), (k_max, 0.0), (q_exp, 0.0), (k_exp, TWO_BF16_ONES))
            for i, (operand, value) in enumerate(pads):
                words = operand.rearrange("p c h t -> p (c h t)").bitcast(F32)
                if i:
                    pool.wait_ge(const["pads"], 2 * i)
                pool.memset(words[32:64, :], value).then_inc(const["pads"], 1)
                pool.wait_ge(const["pads"], 2 * i + 1)
                pool.memset(words[64:128, :], value).then_inc(const["pads"], 1)
            pool.wait_ge(const["pads"], 8)

        def pool_low(pool):
            s = att["b"]
            for c in range(CHUNKS):
                for w in range(2):
                    pool.wait_ge(s["mid"], 2 * c + w + 1)
                    pool.tensor_tensor(parts[:, c, w, 2, :], rest[:, c % 2, w, :], parts[:, c, w, 1, :],
                                       ALU.subtract).then_inc(s["low"], 1)

        def pool_quads(pool, kind):
            s = att[kind]

            def split(k, c):
                done = (k * CHUNKS + c) * 3
                pool.wait_ge(s["folded"], k * CHUNKS + c + 1)
                pool.tensor_tensor(max_split[:, 0, :], row_max[:, :], zeros[:, :], ALU.add).then_inc(s["split"], 1)
                pool.wait_ge(s["split"], done + 1)
                pool.tensor_tensor(max_rest[:, :], row_max[:, :], max_split[:, 0, :], ALU.subtract).then_inc(s["split"], 1)
                pool.wait_ge(s["split"], done + 2)
                pool.tensor_tensor(max_split[:, 1, :], max_rest[:, :], zeros[:, :], ALU.add).then_inc(s["split"], 1)
                pool.wait_ge(s["split"], done + 3)
                pool.tensor_tensor(max_split[:, 2, :], max_rest[:, :], max_split[:, 1, :], ALU.subtract).then_inc(s["max_split"], 1)

            def slot(stretch, q):
                for n, (c, kt) in enumerate(UNITS):
                    for ahead in range(2):
                        for done in range(CHUNKS):
                            if n + LEAD == FIRST[done + 1] + SPLIT_LAG + ahead * NU and (stretch == MIDDLE or ahead == (stretch == OPENING)):
                                split(q + ahead, done)
                    if stretch == OPENING:
                        continue
                    if kt >= TPC * c:
                        pool.wait_ge(s["exp"], q * 2 * NU + 2 * n + 2)
                        pool.wait_ge(s["kept"], q * diagonals(NU) + diagonals(n) + 1)
                        pool.tensor_tensor(carry[:, :], carry[:, :], carry[:, :], ALU.mult)
                        diagonal = probs[:, SLOT[n], :, 0:P]
                        pool.affine_select(out=diagonal, in_=diagonal, compare_op=ALU.is_ge, fill=0.0, base=0,
                                           pattern=[[0, QUAD], [1, P]], channel_multiplier=-1).then_inc(s["kept"], 1)
                    if kind == "b" and n in SUMMED and kt > 0:
                        before = SUMMED[SUMMED.index(n) - 1]
                        pool.wait_ge(s["exp"], q * 2 * NU + 2 * n + 2)
                        if UNITS[before][1] == 0:
                            pool.wait_ge(s["pv"], q * NU + FIRST[c])
                            first = probs[:, SLOT[before], :, :]
                        else:
                            pool.wait_ge(s["summed"], q * adds(NU) + adds(n))
                            first = prob_sum
                        pool.tensor_tensor(prob_sum, first, probs[:, SLOT[n], :, :], ALU.add).then_inc(s["summed"], 1)

            if kind == "b":
                pool.wait_ge(s["x_plus"], 2 * CHUNKS)
            pool.memset(carry[:, :], 0.0).then_inc(s["kept"], 1)
            slot(OPENING, -1)
            with pool.Fori(0, QUADS - 1) as q:
                slot(MIDDLE, q)
            slot(CLOSING, QUADS - 1)

        def pool_plus_bias(pool, i):
            s = ffn[i]
            for c in range(CHUNKS):
                pool.wait_ge(s["y"], TPC * (c + 1))
                pool.tensor_tensor(x_c[c], x_c[c], b2_sum[:, :, :].to_broadcast([P, TPC, D]),
                                   ALU.add).then_inc(s["x_bias"], 1)

        @block.gpsimd
        def _(pool):
            pool.memset(ones[:, :], 1.0).then_inc(const["ones"], 1)
            pool.memset(carry[:, :], 0.0)
            pool.memset(max_split[:, :, :], 0.0).then_inc(const["zero"], 1)
            pool.memset(zeros[:, :], 0.0).then_inc(const["zero"], 1)
            pool.memset(above[:, :], 0.0).then_inc(const["zero"], 1)
            pool.wait_ge(const["zero"], 3)
            pool.wait_ge(const["ones"], 1)
            pool.affine_select(out=ident[:, :], in_=ones[:, :], compare_op=ALU.is_equal, fill=0.0, base=0,
                               pattern=[[1, P]], channel_multiplier=-1).then_inc(const["ident"], 1)
            pool.affine_select(out=above[:, :], in_=above[:, :], compare_op=ALU.is_ge, fill=-3e38, base=0,
                               pattern=[[-1, P]], channel_multiplier=1).then_inc(const["above"], 1)
            pool.wait_ge(const["ident"], 1)
            pool.tensor_copy(ident_b[:, :], ident[:, :]).then_inc(const["ident"], 1)
            pool.tensor_copy(by_width[:, :].rearrange("p (d h) -> p d h", h=HEADS),
                             ident[:, :].rearrange("p (h d) -> p d h", h=HEADS)).then_inc(const["ident"], 1)
            pool.memset(v_all[:, :, :], 1.0).then_inc(const["v_ones"], 1)
            pool.wait_ge(const["v_ones"], 1)
            pool_pads(pool)
            pool.wait_ge(load["w_ffn"], LOAD_WEIGHTS_FFN)
            pool.tensor_tensor(b2_sum[:, 0, :], b2_sb[:, 0, :], b2_sb[:, 1, :], ALU.add).then_inc(const["b2"], 1)
            pool.wait_ge(const["b2"], 1)
            pool.tensor_tensor(b2_sum[:, 0, :], b2_sum[:, 0, :], b2_sb[:, 2, :], ALU.add).then_inc(const["b2"], 1)
            pool.tensor_tensor(gate_sb[:, 1:2], gate_sb[:, 1:2], gate_sb[:, 0:1], ALU.subtract).then_inc(const["gate"], 1)
            pool.wait_ge(const["gate"], 1)
            pool.tensor_scalar(gate_diff[:, :], ones[:, :], gate_sb[:, 1:2], None, ALU.mult).then_inc(const["gate"], 1)
            pool_quads(pool, "a")
            pool.wait_ge(const["b2"], 2)
            pool_plus_bias(pool, 0)
            pool_low(pool)
            pool.wait_ge(load["w_b"], LOAD_WEIGHTS_B)
            for c in range(CHUNKS):
                pool.wait_ge(att["b"]["y"], TPC * (c + 1))
                pool.tensor_tensor(x_c[c], x_c[c], y_c[c], ALU.add).then_inc(att["b"]["x_plus"], 1)
                pool.wait_ge(att["b"]["x_plus"], 2 * c + 1)
                pool.tensor_tensor(x_c[c], x_c[c], bf_sb[:, :].rearrange("p (t d) -> p t d", t=1).to_broadcast([P, TPC, D]),
                                   ALU.add).then_inc(att["b"]["x_plus"], 1)
            pool_quads(pool, "b")
            pool_plus_bias(pool, 1)

        def pe_turn(pe, s, c, to):
            pe.wait_ge(s["y"], TPC * (c + 1))
            for t in range(TPC):
                last = nc.tensor.transpose(tiles_of(bank[to])[:, t, :], y[:, TPC * c + t, :], ident[:, :])
            last.then_inc(s["turned"], 1)

        def pe_project(pe, kind):
            s = att[kind]
            if kind == "a":
                pe.wait_ge(const["ident"], 1)
                pe.wait_ge(load["w_qkv"], 16)
            else:
                pe.wait_ge(load["w_b"], LOAD_WEIGHTS_B)
                pe.wait_ge(const["ident"], 3)
                pe.wait_ge(ffn[0]["out"], CHUNKS - 1)
            for c in range(CHUNKS):
                if c >= 1:
                    pe.wait_ge(s["yT"], c)
                pe_turn(pe, s, c, 0)
                tokens = yT[:, c * CHUNK:(c + 1) * CHUNK]
                if c >= 1:
                    pe.wait_ge(s["rest"], 2 * c)
                pe.wait_ge(s["yT"], c + 1)
                if kind == "a":
                    nc.tensor.matmul(bank[2], w_qkv_sb[:, 0:D], tokens, start=True, stop=True).then_inc(s["qk"], 1)
                    nc.tensor.matmul(bank[3], w_qkv_sb[:, D:2 * D], tokens, start=True, stop=True).then_inc(s["qk"], 1)
                    if c >= 1:
                        pe.wait_ge(s["v_stored"], c)
                    for t in range(TPC):
                        last = nc.tensor.matmul(tiles_of(bank[4])[:, t, :], tokens[:, t * P:(t + 1) * P],
                                                w_qkv_sb[:, 2 * D:3 * D], start=True, stop=True)
                    last.then_inc(s["v"], 1)
                else:
                    nc.tensor.matmul(bank[2], by_width[:, :], tokens, start=True, stop=True).then_inc(s["qk"], 1)
                    if c == 0:
                        pe.wait_ge(ffn[0]["out"], CHUNKS)
                    nc.tensor.matmul(bank[3], w_k_sb[:, :], tokens, start=True, stop=True).then_inc(s["qk"], 1)
                    for t in range(TPC):
                        if c >= 1:
                            pe.wait_ge(s["v_stored"], TPC * (c - 1) + t + 1)
                        nc.tensor.matmul(bank[4 + t], tokens[:, t * P:(t + 1) * P], w_v_sb,
                                         start=True, stop=True).then_inc(s["v"], 1)

        def pe_quads(pe, kind):
            s = att[kind]

            size = 8 - RING[kind]

            def ring_turn(stretch, base, e):
                if not early(stretch, e, size):
                    pe.wait_ge(s["ring_free"], base + e + 1 - size)
                return ring_bank(kind, stretch, e)

            def maxima(stretch, k, base, e, n, h):
                c, kc, i = COMBO[n]
                if n == FIRST[c] and h == 0:
                    pe.wait_ge(s[f"m{c}"], k * 32 + 32)
                w = CHUNK if kc < c else (i + 1) * P
                to = ring_turn(stretch, base, e)
                last = nc.tensor.matmul(to[:, 0:w], q_max[:, c, h, i * P:(i + 1) * P],
                                        k_max[:, kc, h, 0:w], start=True, stop=kc < c)
                if kc == c:
                    last = nc.tensor.matmul(to[:, w - P:w], ident_b[:, :], above[:, :], start=False, stop=True)
                last.then_inc(s["ring_full"], 1)

            def turn(stretch, k, base, e, c):
                pe.wait_ge(s["max_split"], k * CHUNKS + c + 1)
                to = ring_turn(stretch, base, e)
                nc.tensor.transpose(to.bitcast(BF16)[:, 0:P], max_split[:, :, :].rearrange("p a b -> p (a b)"),
                                    ident_b[:, :]).then_inc(s["ring_full"], 1)

            def scores(q, n, pair):
                c, kt = UNITS[n]
                w, o = width(c, kt)
                if kt == 0 and pair == 0:
                    pe.wait_ge(s[f"s{c}"], q * 48 + 48)
                    pe.wait_ge(s[f"r{c}"], q * 16 + 16)
                if n >= 1:
                    pe.wait_ge(s["exp"], q * 2 * NU + 2 * (n - 1) + pair + 1)
                for h in (2 * pair, 2 * pair + 1):
                    last = nc.tensor.matmul(bank[SCORE + h][:, 0:w], k_exp[:, kt // TPC, h, kt % TPC * P:(kt % TPC + 1) * P],
                                            q_exp[:, c, h, o:CHUNK], start=True, stop=True)
                last.then_inc(s["scores"], 1)

            def values(q, n):
                c, kt = UNITS[n]
                w, o = width(c, kt)
                pe.wait_ge(s["exp"], q * 2 * NU + 2 * n + 2)
                if kt >= TPC * c:
                    pe.wait_ge(s["kept"], q * diagonals(NU) + diagonals(n) + 2)
                if kt == 0:
                    pe.wait_ge(s["sums"], q * CHUNKS + c + 1)
                ends = kt == TPC * (c + 1) - 1
                for h in range(QUAD):
                    last = nc.tensor.matmul(bank[PV][32 * h:32 * h + 32, o:CHUNK], v_quad[:, kt, VW * h:VW * (h + 1)],
                                            probs[:, SLOT[n], h, 0:w], start=kt == 0, stop=ends)
                if kind == "a" or n in SUMMED:
                    last.then_inc(s["pv"], 1)

            def denominators(q, n):
                c, kt = UNITS[n]
                w, o = width(c, kt)
                ends = kt == TPC * (c + 1) - 1
                if kind == "a" or n in SUMMED:
                    return
                starts = all(m in SUMMED for m in range(FIRST[c], n))
                for h in range(QUAD):
                    last = nc.tensor.matmul(bank[DEN][32 * h:32 * h + 32, o:CHUNK], ones[:, 0:VW],
                                            probs[:, SLOT[n], h, 0:w], start=starts, stop=ends and c == 0)
                if ends and c >= 1:
                    pe.wait_ge(s["summed"], q * adds(NU) + adds(n))
                    for h in range(QUAD):
                        last = nc.tensor.matmul(bank[DEN][32 * h:32 * h + 32, :], ones[:, 0:VW],
                                                prob_sum[:, h, :], start=False, stop=True)
                last.then_inc(s["pv"], 1)

            def out_turn(stretch, q, base, e, c, which):
                pe.wait_ge(s["sums"], q * CHUNKS + c + 2)
                to = ring_turn(stretch, base, e)
                for t in range(TPC):
                    last = nc.tensor.transpose(tiles_of(to)[:, t, :], sums[:, which, t * P:(t + 1) * P],
                                               ident[:, :])
                last.then_inc(s["ring_full"], 1)

            def slot(stretch, q):
                place = ring(kind, stretch)
                base = ring_base(kind, stretch, q)
                for step in order(kind, stretch):
                    what, ahead, n, h = step
                    if what == "max":
                        maxima(stretch, q + ahead, base, place[step], n, h)
                    elif what == "turn":
                        turn(stretch, q + ahead, base, place[step], n)
                    elif what == "scores":
                        scores(q, n, h)
                    elif what == "values":
                        values(q, n)
                    elif what == "ones":
                        denominators(q, n)
                    else:
                        out_turn(stretch, q, base, place[step], n, int(what == "den"))

            if kind == "a":
                pe.wait_ge(const["ident"], 2)
                pe.wait_ge(const["ones"], 1)
                pe.wait_ge(const["above"], 1)
            pe.wait_ge(s["rest"], 2 * CHUNKS)
            pe.wait_ge(s["v_stored"], TILES if kind == "b" else CHUNKS)
            slot(OPENING, -1)
            with pe.Fori(0, QUADS - 1) as q:
                slot(MIDDLE, q)
            slot(CLOSING, QUADS - 1)

        def pe_out(pe, kind):
            s = att[kind]
            groups = 1 if kind == "a" else QUADS
            pe.wait_ge(load["w_o" if kind == "a" else "w_f"], 16)

            def turn_back(c):
                pe.wait_ge(s["o"], 1 + (QUADS - 1) * CHUNKS + c + 1)
                for g in range(groups):
                    if c == 0 and 4 + g == RING[kind]:
                        pe.wait_ge(s["o"], 1 + QUADS * CHUNKS)
                    if c >= 1:
                        pe.wait_ge(s["o_turned"], groups * (c - 1) + g + 1)
                    for t in range(TPC):
                        last = nc.tensor.transpose(tiles_of(bank[4 + g])[:, t, :],
                                                   o_tok[:, TPC * c + t, g * D:(g + 1) * D], ident[:, :])
                    last.then_inc(s["o_back"], 1)

            turn_back(0)
            for c in range(CHUNKS):
                if c < CHUNKS - 1:
                    turn_back(c + 1)
                pe.wait_ge(s["o_turned"], groups * (c + 1))
                for t in range(TPC):
                    for g in range(groups):
                        last = nc.tensor.matmul(tiles_of(bank[c])[:, t, :], turned_o[:, c % 2, g, t * P:(t + 1) * P],
                                                w_out_sb[:, g, :], start=g == 0, stop=g == groups - 1)
                last.then_inc(s["projected"], 1)

        def pe_ffn(pe, i):
            s = ffn[i]
            pe.wait_ge(load["w_ffn"], LOAD_WEIGHTS_FFN)
            pe.wait_ge(const["gate"], 2)
            before = att["ab"[i]]
            pe.wait_ge(before["x_done"], 2)

            def turn_and_gate(c):
                pe_turn(pe, s, c, 0)
                pe.wait_ge(s["yT"], c + 1)
                nc.tensor.matmul(bank[1], gate_diff[:, :], yT[:, c * CHUNK:(c + 1) * CHUNK],
                                 start=True, stop=True).then_inc(s["gate"], 1)

            turn_and_gate(0)
            for c in range(CHUNKS):
                for m in range(HCH):
                    e, j = divmod(m, HID // P)
                    u = c * HCH + m
                    if u >= 4:
                        pe.wait_ge(s["up_act" if u % 2 == 0 else "up_dve"], (u - 4) // 2 + 1)
                    if m == HID // P:
                        pe.wait_ge(s["masked"], 2 * (c + 1))
                    if e == 0:
                        tokens = yT[:, c * CHUNK:(c + 1) * CHUNK]
                    else:
                        tokens = masked[:, c % 2, e - 1, :]
                    nc.tensor.matmul(bank[4 + u % 4], w1_sb[:, e, j * P:(j + 1) * P], tokens,
                                     start=True, stop=True).then_inc(s["up"], 1)
                if c < CHUNKS - 1:
                    turn_and_gate(c + 1)
                pe.wait_ge(s["up_act"], HCH // 2 * (c + 1))
                pe.wait_ge(s["up_dve"], HCH // 2 * (c + 1))
                if c == 0:
                    pe.wait_ge(before["x_done"], CHUNKS)
                if c >= 2:
                    pe.wait_ge(s["out"], c - 1)
                for t in range(TPC):
                    for m in range(HCH):
                        last = nc.tensor.matmul(tiles_of(bank[2 + c % 2])[:, t, :], hidden[c % 2][:, m, t * P:(t + 1) * P],
                                                w2_sb[:, m, :], start=m == 0, stop=m == HCH - 1)
                last.then_inc(s["down"], 1)

        @block.tensor
        def _(pe):
            pe_project(pe, "a")
            pe_quads(pe, "a")
            pe_out(pe, "a")
            pe_ffn(pe, 0)
            pe_project(pe, "b")
            pe_quads(pe, "b")
            pe_out(pe, "b")
            pe_ffn(pe, 1)

        def act_sqrt(act, s, c):
            act.wait_ge(s["norm"], NORM_STEPS * c + 2 * TPC + 1)
            nc.scalar.activation(deviation[:, TPC * c:TPC * (c + 1)], rstd[:, TPC * c:TPC * (c + 1)],
                                 ACT.Sqrt).then_inc(s["sqrt"], 1)

        def act_store_yT(act, s, c):
            act.wait_ge(s["turned"], c + 1)
            nc.scalar.copy(yT[:, c * CHUNK:(c + 1) * CHUNK], bank[0]).then_inc(s["yT"], 1)

        def act_project(act, kind):
            s = att[kind]
            v_heads = v_all[:, :, :].rearrange("p t (h w) -> p t h w", h=HEADS)

            def high(c, w):
                act.wait_ge(s["qk"], 2 * c + w + 1)
                source = bank[2 + w]
                if kind == "b" and w == 1:
                    nc.scalar.activation(parts[:, c, w, 0, :], source, ACT.Identity, bias=bk_sb[:, 0:1]).then_inc(s["high"], 1)
                else:
                    nc.scalar.copy(parts[:, c, w, 0, :], source).then_inc(s["high"], 1)

            if kind == "a":
                act_sqrt(act, s, 0)
                act_sqrt(act, s, 1)
            else:
                act_sqrt(act, s, CHUNKS - 1)
            for c in range(CHUNKS):
                act_store_yT(act, s, c)
                high(c, 0)
                high(c, 1)
                if kind == "a":
                    if c == 0:
                        act.wait_ge(const["v_ones"], 1)
                    act.wait_ge(s["v"], c + 1)
                    nc.scalar.copy(v_heads[:, TPC * c:TPC * (c + 1), :, 0:HD],
                                   bank[4].rearrange("p (t h d) -> p t h d", t=TPC, h=HEADS)).then_inc(s["v_stored"], 1)
                for w in range(2):
                    act.wait_ge(s["rest"], 2 * c + w + 1)
                    nc.scalar.copy(parts[:, c, w, 1, :], rest[:, c % 2, w, :]).then_inc(s["mid"], 1)
                if kind == "a" and c + 2 < CHUNKS:
                    act_sqrt(act, s, c + 2)

        def act_quads(act, kind):
            s = att[kind]
            scale = HD ** -0.5 if kind == "a" else 1.0

            def copy_sums(q, c):
                act.wait_ge(s["pv"], q * NU + FIRST[c + 1])
                act.wait_ge(s["o"], q * CHUNKS + c + 1)
                banks = 1 if kind == "a" else 2
                nc.scalar.copy(sums[:, 0:banks, :], psum[:, PV:PV + banks, :]).then_inc(s["sums"], 1)

            def quad(q):
                for n, (c, kt) in enumerate(UNITS):
                    w, o = width(c, kt)
                    for pair in range(2):
                        act.wait_ge(s["scores"], q * 2 * NU + 2 * n + pair + 1)
                        if pair == 0 and SLOT[n] in SLOT[:n]:
                            last = max(m for m in range(n) if SLOT[m] == SLOT[n])
                            act.wait_ge(s["pv"], q * NU + last + 1)
                            if kind == "b" and last in SUMMED:
                                added = last + 1 if UNITS[last][1] > 0 else last + 2
                                act.wait_ge(s["summed"], q * adds(NU) + adds(added))
                        heads = slice(2 * pair, 2 * pair + 2)
                        nc.scalar.activation(probs[:, SLOT[n], heads, 0:w], psum[:, SCORE + 2 * pair:SCORE + 2 * pair + 2, 0:w],
                                             ACT.Exp, scale=scale).then_inc(s["exp"], 1)
                    if n in FIRST[1:]:
                        copy_sums(q, FIRST.index(n) - 1)
                copy_sums(q, CHUNKS - 1)

            nc.scalar.copy(act_word[:, :], ones[0:1, 0:1]).then_inc(s["sums"], 1)
            act.wait_ge(s["low"], 2 * CHUNKS)
            for c in range(CHUNKS):
                act.wait_ge(s[f"rows{c}"], 2 * PARTS * 16)
            with act.Fori(0, QUADS) as q:
                quad(q)

        def act_out(act, kind):
            s = att[kind]
            groups = 1 if kind == "a" else QUADS
            for c in range(CHUNKS):
                for g in range(groups):
                    act.wait_ge(s["o_back"], groups * c + g + 1)
                    if c >= 2 and g == 0:
                        act.wait_ge(s["projected"], c - 1)
                    nc.scalar.activation(turned_o[:, c % 2, g, :], bank[4 + g],
                                         ACT.Gelu if kind == "b" else ACT.Copy).then_inc(s["o_turned"], 1)

        def act_ffn(act, i):
            s = ffn[i]
            for c in range(CHUNKS):
                act_sqrt(act, s, c)
            act_store_yT(act, s, 0)
            for c in range(CHUNKS):
                if c >= 2:
                    act.wait_ge(s["down"], c - 1)
                for m in range(0, HCH, 2):
                    u = c * HCH + m
                    act.wait_ge(s["up"], u + 1)
                    nc.scalar.activation(hidden[c % 2][:, m, :], bank[4 + u % 4], ACT.Relu,
                                         bias=b1_sb[:, m:m + 1]).then_inc(s["up_act"], 1)
                if c < CHUNKS - 1:
                    act_store_yT(act, s, c + 1)
                if i == 0 and c >= 1:
                    act_sqrt(act, att["b"], c - 1)

        @block.scalar
        def _(act):
            act_project(act, "a")
            act_quads(act, "a")
            act_out(act, "a")
            act_ffn(act, 0)
            act_project(act, "b")
            act_quads(act, "b")
            act_out(act, "b")
            act_ffn(act, 1)

        def dve_statistics(dve, s, c):
            tiles = range(TPC * c, TPC * (c + 1))
            for t in tiles:
                nc.vector.bn_stats(stats[:, t, :], x[:, t, :]).then_inc(s["norm"], 1)
            for t in tiles:
                dve.wait_ge(s["norm"], NORM_STEPS * c + t - TPC * c + 1)
                nc.vector.bn_aggr(mean_var[:, t, :], stats[:, t, :]).then_inc(s["norm"], 1)
            dve.wait_ge(s["norm"], NORM_STEPS * c + 2 * TPC)
            nc.vector.tensor_scalar(rstd[:, TPC * c:TPC * (c + 1)], mean_var[:, TPC * c:TPC * (c + 1), 1], EPS, None,
                                    ALU.add).then_inc(s["norm"], 1)

        def dve_normalise(dve, s, c):
            dve.wait_ge(s["sqrt"], c + 1)
            nc.vector.reciprocal(rstd[:, TPC * c:TPC * (c + 1)], deviation[:, TPC * c:TPC * (c + 1)]).then_inc(s["rstd"], 1)
            dve.wait_ge(s["rstd"], c + 1)
            for t in range(TPC * c, TPC * (c + 1)):
                nc.vector.tensor_scalar(y[:, t, :], x[:, t, :], mean_var[:, t, 0:1], rstd[:, t:t + 1],
                                        ALU.subtract, ALU.mult).then_inc(s["y"], 1)

        def dve_project(dve, kind):
            s = att[kind]
            if kind == "a":
                for c in range(2):
                    dve.wait_ge(load[f"x{c}"], 16)
                    dve_statistics(dve, s, c)
                    dve_normalise(dve, s, c)
            else:
                dve_normalise(dve, s, CHUNKS - 1)
            for c in range(CHUNKS):
                for w in range(2):
                    dve.wait_ge(s["high"], 2 * c + w + 1)
                    if c >= 2:
                        dve.wait_ge(s["low"], 2 * (c - 2) + w + 1)
                    if kind == "b" and w == 1:
                        nc.vector.scalar_tensor_tensor(rest[:, c % 2, w, :], bank[3], bk_sb[:, 0:1], parts[:, c, w, 0, :],
                                                       ALU.add, ALU.subtract).then_inc(s["rest"], 1)
                    else:
                        nc.vector.tensor_tensor(rest[:, c % 2, w, :], bank[2 + w], parts[:, c, w, 0, :],
                                                ALU.subtract).then_inc(s["rest"], 1)
                if kind == "b":
                    for t in range(TPC):
                        dve.wait_ge(s["v"], TPC * c + t + 1)
                        nc.vector.tensor_tensor(v_all[:, TPC * c + t, :], bank[4 + t], bv_sb, ALU.add
                                                ).then_inc(s["v_stored"], 1)
                if kind == "a" and c + 2 < CHUNKS:
                    dve.wait_ge(load[f"x{c + 2}"], 16)
                    dve_statistics(dve, s, c + 2)
                    dve_normalise(dve, s, c + 2)
                if kind == "a":
                    for w in range(2):
                        dve.wait_ge(s["mid"], 2 * c + w + 1)
                        nc.vector.tensor_tensor(parts[:, c, w, 2, :], rest[:, c % 2, w, :], parts[:, c, w, 1, :],
                                                ALU.subtract).then_inc(s["low"], 1)

        def dve_quads(dve, kind):
            s = att[kind]

            def maxima(stretch, k, base, e, n, h):
                c, kc, i = COMBO[n]
                if n == FIRST[c] and h == 0 and not (isinstance(k, int) and k == 0 and c == 0):
                    dve.wait_ge(s["folded"], k * CHUNKS + c)
                w = CHUNK if kc < c else (i + 1) * P
                dve.wait_ge(s["ring_full"], base + e + 1)
                nc.vector.tensor_reduce(max_parts[:, h, i, kc:kc + 1], ring_bank(kind, stretch, e)[:, 0:w],
                                        AX.X, ALU.max).then_inc(s["ring_free"], 1)
                if n + 1 in FIRST and h == QUAD - 1:
                    fold(k, c, base + e + 1)

            def fold(k, c, entries):
                dve.wait_ge(s["ring_free"], entries)
                nc.vector.tensor_reduce(row_max[:, :].rearrange("p (h i) -> p h i", h=QUAD), max_parts[:, :, :, 0:c + 1],
                                        AX.X, ALU.max).then_inc(s["folded"], 1)

            def turn(stretch, k, base, e, c):
                dve.wait_ge(s["ring_full"], base + e + 1)
                if not (isinstance(k, int) and k == 0):
                    dve.wait_ge(s[f"r{c}"], k * 16)
                nc.vector.tensor_scalar(max_rows[:, c, :], ring_bank(kind, stretch, e).bitcast(BF16)[0:PARTS * QUAD * TPC, 0:P],
                                        -1.0, None, ALU.mult).then_inc(s["ring_free"], 1)

            def denominators(stretch, q, base, e, c):
                dve.wait_ge(s["ring_full"], base + e + 1)
                dve.wait_ge(s["o"], q * CHUNKS + c + 1)
                column = HD if kind == "a" else 0
                inverse = nc.vector.reciprocal(recip[:, :, :, :], ring_bank(kind, stretch, e).rearrange(
                    "p (t h d) -> p t h d", t=TPC, h=QUAD)[:, :, :, column:column + 1])
                if kind == "a":
                    inverse.then_inc(s["recip"], 1)
                else:
                    inverse.then_inc(s["ring_free"], 1)

            def normalise(stretch, q, base, e, c):
                wide = HD if kind == "a" else VW
                if kind == "a":
                    denominators(stretch, q, base, e, c)
                    dve.wait_ge(s["recip"], q * CHUNKS + c + 1)
                else:
                    dve.wait_ge(s["ring_full"], base + e + 1)
                    dve.wait_ge(s["ring_free"], base + e)
                values = ring_bank(kind, stretch, e).rearrange("p (t h d) -> p t h d", t=TPC, h=QUAD)[:, :, :, 0:wide]
                o = o_tok[:, TPC * c:TPC * (c + 1), bass.ds(q * QUAD * wide, QUAD * wide)]
                nc.vector.tensor_tensor(o.rearrange("p t (h d) -> p t h d", h=QUAD), values,
                                        recip[:, :, :, :].to_broadcast([P, TPC, QUAD, wide]), ALU.mult).then_inc(s["o"], 1)
                dve.wait_ge(s["o"], q * CHUNKS + c + 2)
                nc.vector.memset(dve_word[:, :], 0.0).then_inc(s["ring_free"], 1)

            def slot(stretch, q):
                base = ring_base(kind, stretch, q)
                for step, e in ring(kind, stretch).items():
                    what, ahead, n, h = step
                    if what == "max":
                        maxima(stretch, q + ahead, base, e, n, h)
                    elif what == "turn":
                        turn(stretch, q + ahead, base, e, n)
                    elif what == "den":
                        denominators(stretch, q, base, e, n)
                    else:
                        normalise(stretch, q, base, e, n)

            if kind == "a":
                dve.wait_ge(const["b2"], 2)
            nc.vector.memset(dve_word[:, :], 0.0).then_inc(s["o"], 1)
            slot(OPENING, -1)
            with dve.Fori(0, QUADS - 1) as q:
                slot(MIDDLE, q)
            slot(CLOSING, QUADS - 1)

        def dve_add(dve, s, c, done, count, source):
            dve.wait_ge(s[done], count)
            return nc.vector.tensor_tensor(x_c[c], tiles_of(source), x_c[c], ALU.add)

        def dve_after(dve, i):
            s = att["ab"[i]]
            for c in range(CHUNKS):
                dve_add(dve, s, c, "projected", c + 1, bank[c]).then_inc(s["x_done"], 1)
                dve.wait_ge(s["x_done"], c + 1)
                dve_statistics(dve, ffn[i], c)
                if c == CHUNKS - 2:
                    dve_normalise(dve, ffn[i], 0)

        def dve_ffn(dve, i):
            s = ffn[i]
            for c in range(1, CHUNKS):
                dve_normalise(dve, s, c)

            def mask(c):
                dve.wait_ge(s["gate"], c + 1)
                tokens = yT[:, c * CHUNK:(c + 1) * CHUNK]
                for e, chooses in enumerate((ALU.is_le, ALU.is_gt)):
                    nc.vector.scalar_tensor_tensor(masked[:, c % 2, e, :], bank[1], 0.0, tokens,
                                                   chooses, ALU.mult).then_inc(s["masked"], 1)

            mask(0)
            for c in range(CHUNKS):
                if c >= 2:
                    dve.wait_ge(s["down"], c - 1)
                for m in range(1, HCH, 2):
                    u = c * HCH + m
                    dve.wait_ge(s["up"], u + 1)
                    nc.vector.tensor_scalar(hidden[c % 2][:, m, :], bank[4 + u % 4], b1_sb[:, m:m + 1], 0.0,
                                            ALU.add, ALU.max).then_inc(s["up_dve"], 1)
                if c < CHUNKS - 1:
                    mask(c + 1)
                dve.wait_ge(s["x_bias"], c + 1)
                dve_add(dve, s, c, "down", c + 1, bank[2 + c % 2]).then_inc(s["out"], 1)
                if i == 0:
                    dve.wait_ge(s["out"], c + 1)
                    dve_statistics(dve, att["b"], c)
                    if c >= 1:
                        dve_normalise(dve, att["b"], c - 1)

        @block.vector
        def _(dve):
            dve_project(dve, "a")
            dve_quads(dve, "a")
            dve_after(dve, 0)
            dve_ffn(dve, 0)
            dve_project(dve, "b")
            dve_quads(dve, "b")
            dve.wait_ge(att["b"]["x_plus"], 2 * CHUNKS)
            dve_after(dve, 1)
            dve_ffn(dve, 1)


def kernel(**inputs):
    from concourse import bacc
    from concourse.bass_utils import run_bass_kernel_spmd

    a = {k: np.ascontiguousarray(v) for k, v in inputs.items()}

    def by_width(w):
        return w.reshape(w.shape[0], HEADS, HD).transpose(0, 2, 1).reshape(w.shape)

    w_qkv = a["L0_attn_a_w_qkv"].T
    arrays = {
        "x_in": a["L0_attn_a_x"].reshape(S, D),
        "wqkvT": np.concatenate([by_width(w_qkv[:, :D]), by_width(w_qkv[:, D:2 * D]), w_qkv[:, 2 * D:]], 1),
        "woT": a["L0_attn_a_w_out"].T,
        "wk": by_width(a["L0_attn_b_Wk"]),
        "bk": by_width(a["L0_attn_b_bk"].reshape(1, D)).T,
        "wv": a["L0_attn_b_Wv"],
        "bv": a["L0_attn_b_bv"],
        "wf": a["L0_attn_b_Wf"],
        "bf": a["L0_attn_b_bf"],
        "gateT": a["L0_ffn_gate_w"].T,
        "w1": np.concatenate([a["L0_ffn_sw1"][None], a["L0_ffn_w1"]]),
        "b1": np.concatenate([a["L0_ffn_sb1"][None], a["L0_ffn_b1"]]).reshape(HCH, P).T,
        "w2": np.concatenate([a["L0_ffn_sw2"], a["L0_ffn_w2"].reshape(-1, D)]),
        "b2": np.concatenate([a["L0_ffn_sb2"][None], a["L0_ffn_b2"]]),
    }
    nc = bacc.Bacc("TRN2", target_bir_lowering=False, num_devices=1)
    maps, args = {}, []
    for name, array in arrays.items():
        array = np.ascontiguousarray(array)
        maps[f"in_{name}"] = array
        args.append(nc.dram_tensor(f"in_{name}", array.shape, mybir.dt.from_np(array.dtype), kind="ExternalInput").ap())
    out = nc.dram_tensor("out_x", (S, D), F32, kind="ExternalOutput").ap()
    build(nc, *args, out)
    result = run_bass_kernel_spmd(nc, [maps], core_ids=[0])
    return result.results[0]["out_x"].reshape(1, S, D)
```
